# Optimizing a Trainium2 kernel written in Bass

```python
import numpy as np
import jax
import jax.numpy as jnp

def _softmax(x, axis=-1):
    return jax.nn.softmax(x, axis=axis)

def _gelu(x):
    return jax.nn.gelu(x, approximate=True)

def _silu(x):
    return jax.nn.silu(x)

def _sigmoid(x):
    return jax.nn.sigmoid(x)

def _layernorm(x, axis=-1, eps=1e-05):
    m = jnp.mean(x, axis=axis, keepdims=True)
    v = jnp.var(x, axis=axis, keepdims=True)
    return (x - m) / jnp.sqrt(v + eps)

def _scatter_add(tgt, idx, src, axis=0):
    return tgt.at[idx].add(src)

def _segment_sum(src, seg, n):
    return jax.ops.segment_sum(src, seg, n)
kernel_name = 'mk_hybrid_d1_jaxref_r8_d9f480'

def setup_inputs(seed: int=0):
    np.random.seed(seed)
    _w = jnp.asarray

    def _L0_attn_a_setup():
        import jax, jax.numpy as jnp
        import numpy as np
        B, S, D, H = (2, 256, 128, 16)
        HD = D // H
        key = jax.random.key(seed)
        ks = jax.random.split(key, 5)
        scale = 1.0 / np.sqrt(D)
        x = jax.random.normal(ks[0], (B, S, D), dtype=jnp.float32)
        W_Q = jax.random.uniform(ks[1], (D, D), jnp.float32, -scale, scale)
        W_K = jax.random.uniform(ks[2], (D, D), jnp.float32, -scale, scale)
        W_V = jax.random.uniform(ks[3], (D, D), jnp.float32, -scale, scale)
        W_O = jax.random.uniform(ks[4], (D, D), jnp.float32, -scale, scale)
        return {'x': x, 'W_Q': W_Q, 'W_K': W_K, 'W_V': W_V, 'W_O': W_O}
    _L0_attn_a_in = _L0_attn_a_setup()

    def _L0_attn_b_setup():
        import jax, jax.numpy as jnp
        import numpy as np
        HEADS = 16
        ROPE_BASE = 10000.0

        def _rope_tables(T, head_dim, dtype):
            half = head_dim // 2
            inv_freq = 1.0 / ROPE_BASE ** (jnp.arange(0, head_dim, 2, dtype=jnp.float32) / head_dim)
            t = jnp.arange(T, dtype=jnp.float32)
            freqs = t[:, None] * inv_freq[None, :]
            cos = jnp.cos(freqs).astype(dtype)[None, None]
            sin = jnp.sin(freqs).astype(dtype)[None, None]
            return (cos, sin)

        def _apply_rope(x, cos, sin):
            xe, xo = jnp.split(x, 2, axis=-1)
            return jnp.concatenate([xe * cos - xo * sin, xe * sin + xo * cos], axis=-1)
        key = jax.random.key(seed)
        k1, k2, k3 = jax.random.split(key, 3)
        B, T, D = (4, 512, 128)
        x = jax.random.normal(k1, (B, T, D), dtype=jnp.float32)
        w_qkv = jax.random.normal(k2, (3 * D, D), dtype=jnp.float32) * 0.02
        w_out = jax.random.normal(k3, (D, D), dtype=jnp.float32) * 0.02
        return {'x': x, 'w_qkv': w_qkv, 'w_out': w_out}
    _L0_attn_b_in = _L0_attn_b_setup()

    def _L0_ffn_setup():
        import jax, jax.numpy as jnp
        import numpy as np
        DIM = 128

        def _reference_tuple_inner(x, W_r, W_k, W_v, mu_r, mu_k):
            B, T, C = x.shape
            x_prev = jnp.concatenate([jnp.zeros((B, 1, C), x.dtype), x[:, :-1, :]], axis=1)
            xr = mu_r * x + (1.0 - mu_r) * x_prev
            xk = mu_k * x + (1.0 - mu_k) * x_prev
            r = jax.nn.sigmoid(jnp.einsum('btc,dc->btd', xr, W_r))
            k = jnp.einsum('btc,dc->btd', xk, W_k)
            k_act = jnp.square(jax.nn.relu(k))
            out = r * jnp.einsum('btc,dc->btd', k_act, W_v)
            new_state = x[:, -1, :]
            return (out, new_state)
        key = jax.random.key(seed)
        ks = jax.random.split(key, 6)
        B, T, C = (8, 256, DIM)
        x = jax.random.normal(ks[0], (B, T, C), dtype=jnp.float32)
        s = 1.0 / np.sqrt(C)
        W_r = jax.random.uniform(ks[1], (C, C), jnp.float32, -s, s)
        W_k = jax.random.uniform(ks[2], (C, C), jnp.float32, -s, s)
        W_v = jax.random.uniform(ks[3], (C, C), jnp.float32, -s, s)
        mu_r = jax.random.uniform(ks[4], (C,), jnp.float32)
        mu_k = jax.random.uniform(ks[5], (C,), jnp.float32)
        return {'x': x, 'W_r': W_r, 'W_k': W_k, 'W_v': W_v, 'mu_r': mu_r, 'mu_k': mu_k}
    _L0_ffn_in = _L0_ffn_setup()
    _d = {'L0_attn_a_x': _L0_attn_a_in['x'], 'L0_attn_a_W_Q': _L0_attn_a_in['W_Q'], 'L0_attn_a_W_K': _L0_attn_a_in['W_K'], 'L0_attn_a_W_V': _L0_attn_a_in['W_V'], 'L0_attn_a_W_O': _L0_attn_a_in['W_O'], 'L0_attn_b_w_qkv': _L0_attn_b_in['w_qkv'], 'L0_attn_b_w_out': _L0_attn_b_in['w_out'], 'L0_ffn_W_r': _L0_ffn_in['W_r'], 'L0_ffn_W_k': _L0_ffn_in['W_k'], 'L0_ffn_W_v': _L0_ffn_in['W_v'], 'L0_ffn_mu_r': _L0_ffn_in['mu_r'], 'L0_ffn_mu_k': _L0_ffn_in['mu_k']}
    _x0 = _d['L0_attn_a_x']
    _d['L0_attn_a_x'] = jax.random.normal(jax.random.fold_in(jax.random.key(seed), 1), (1, 2048, 128), dtype=_x0.dtype)
    del _x0
    return _d

def reference(L0_attn_a_x, L0_attn_a_W_Q, L0_attn_a_W_K, L0_attn_a_W_V, L0_attn_a_W_O, L0_attn_b_w_qkv, L0_attn_b_w_out, L0_ffn_W_r, L0_ffn_W_k, L0_ffn_W_v, L0_ffn_mu_r, L0_ffn_mu_k):

    def _L0_attn_a_ref(x, W_Q, W_K, W_V, W_O):
        import jax, jax.numpy as jnp
        import numpy as np
        B, S, D, H = (2, 256, 128, 16)
        HD = D // H
        b, s, d = x.shape
        Q = (x @ W_Q.T).reshape(b, s, H, HD).transpose(0, 2, 1, 3)
        K = (x @ W_K.T).reshape(b, s, H, HD).transpose(0, 2, 1, 3)
        V = (x @ W_V.T).reshape(b, s, H, HD).transpose(0, 2, 1, 3)
        attn = jnp.einsum('bhqd,bhkd->bhqk', Q, K) / jnp.sqrt(jnp.float32(HD))
        slopes = 1.0 / (2.0 ** 8) ** ((jnp.arange(H, dtype=jnp.float32) + 1) / H)
        pos = jnp.arange(s)
        rel = jnp.minimum(pos[None, :] - pos[:, None], 0).astype(jnp.float32)
        bias = slopes[:, None, None] * rel[None, :, :]
        causal = pos[None, :] <= pos[:, None]
        attn = jnp.where(causal[None, None], attn + bias[None], -jnp.inf)
        attn = jax.nn.softmax(attn, axis=-1)
        out = jnp.einsum('bhqk,bhkd->bhqd', attn, V)
        out = out.transpose(0, 2, 1, 3).reshape(b, s, d)
        return out @ W_O.T

    def _L0_attn_b_ref(x, w_qkv, w_out):
        import jax, jax.numpy as jnp
        import numpy as np
        HEADS = 16
        ROPE_BASE = 10000.0

        def _rope_tables(T, head_dim, dtype):
            half = head_dim // 2
            inv_freq = 1.0 / ROPE_BASE ** (jnp.arange(0, head_dim, 2, dtype=jnp.float32) / head_dim)
            t = jnp.arange(T, dtype=jnp.float32)
            freqs = t[:, None] * inv_freq[None, :]
            cos = jnp.cos(freqs).astype(dtype)[None, None]
            sin = jnp.sin(freqs).astype(dtype)[None, None]
            return (cos, sin)

        def _apply_rope(x, cos, sin):
            xe, xo = jnp.split(x, 2, axis=-1)
            return jnp.concatenate([xe * cos - xo * sin, xe * sin + xo * cos], axis=-1)
        B, T, D = x.shape
        H = HEADS
        hd = D // H
        scale = hd ** (-0.5)
        qkv = (x @ w_qkv.T).reshape(B, T, 3, H, hd)
        qkv = jnp.transpose(qkv, (2, 0, 3, 1, 4))
        q, k, v = (qkv[0], qkv[1], qkv[2])
        cos, sin = _rope_tables(T, hd, x.dtype)
        q = _apply_rope(q, cos, sin)
        k = _apply_rope(k, cos, sin)
        q_feat = jax.nn.elu(q * scale) + 1.0
        k_feat = jax.nn.elu(k) + 1.0
        kv = jnp.einsum('bhtd,bhtv->bhdv', k_feat, v)
        k_sum = k_feat.sum(axis=2)
        denom = jnp.maximum(jnp.einsum('bhtd,bhd->bht', q_feat, k_sum), 1e-06)
        out = jnp.einsum('bhtd,bhdv->bhtv', q_feat, kv) / denom[..., None]
        out = jnp.transpose(out, (0, 2, 1, 3)).reshape(B, T, D)
        return out @ w_out.T

    def _L0_ffn_ref(x, W_r, W_k, W_v, mu_r, mu_k):
        import jax, jax.numpy as jnp
        import numpy as np
        DIM = 128

        def _reference_tuple_inner(x, W_r, W_k, W_v, mu_r, mu_k):
            B, T, C = x.shape
            x_prev = jnp.concatenate([jnp.zeros((B, 1, C), x.dtype), x[:, :-1, :]], axis=1)
            xr = mu_r * x + (1.0 - mu_r) * x_prev
            xk = mu_k * x + (1.0 - mu_k) * x_prev
            r = jax.nn.sigmoid(jnp.einsum('btc,dc->btd', xr, W_r))
            k = jnp.einsum('btc,dc->btd', xk, W_k)
            k_act = jnp.square(jax.nn.relu(k))
            out = r * jnp.einsum('btc,dc->btd', k_act, W_v)
            new_state = x[:, -1, :]
            return (out, new_state)
        return _reference_tuple_inner(x, W_r, W_k, W_v, mu_r, mu_k)[0]
    x = L0_attn_a_x
    x = x + _L0_attn_a_ref(_layernorm(x, axis=-1), L0_attn_a_W_Q, L0_attn_a_W_K, L0_attn_a_W_V, L0_attn_a_W_O)
    x = x + _L0_ffn_ref(_layernorm(x, axis=-1), L0_ffn_W_r, L0_ffn_W_k, L0_ffn_W_v, L0_ffn_mu_r, L0_ffn_mu_k)
    x = x + _L0_attn_b_ref(_layernorm(x, axis=-1), L0_attn_b_w_qkv, L0_attn_b_w_out)
    x = x + _L0_ffn_ref(_layernorm(x, axis=-1), L0_ffn_W_r, L0_ffn_W_k, L0_ffn_W_v, L0_ffn_mu_r, L0_ffn_mu_k)
    return x

_drawn_inputs = setup_inputs


def setup_inputs(seed=0):
    import zlib

    import numpy as np

    out = dict(_drawn_inputs(seed))
    spreads = {}
    factors = {'L0_attn_b_w_qkv': 8.0, 'L0_attn_b_w_out': 8.0, 'L0_ffn_mu_r': 3.133}
    for name, (base, spread) in spreads.items():
        noise = np.random.default_rng([zlib.crc32(name.encode()), seed]).standard_normal(out[name].shape)
        drawn = base * np.exp(spread * noise) if base else spread * noise
        out[name] = jnp.asarray(drawn.astype(out[name].dtype))
    for name, factor in factors.items():
        out[name] = (out[name] * factor).astype(out[name].dtype)
    return out
```

```python
from contextlib import ExitStack

import numpy as np

import concourse.bass as bass
from concourse import mybir

F32 = mybir.dt.float32
BF16 = mybir.dt.bfloat16
I32 = mybir.dt.int32
ALU = mybir.AluOpType
ACT = mybir.ActivationFunctionType
AX = mybir.AxisListType
RMAX = bass.bass_isa.ReduceOp.max

P = 128
T = 2048
D = 128
H = 16
HD = D // H
TILES = T // P
CH = 512
NCH = T // CH
TPC = CH // P
G = H // 4
EPS = 1e-5
PARTS = 3
PAIR_ROWS = PARTS * PARTS * HD
POS_ROWS = 12
SHIFT_ROW = 96
ROWS = SHIFT_ROW + PARTS
CONST_ROWS = ROWS - PAIR_ROWS
SHIFT = 32.0
V1 = HD + 1
VPAD = 24

W_Q, W_K, W_V, W_O, W_R, W_KK, W_VV, W_QKV, W_OUT, MU_R, MU_K = (
    0, 128, 256, 384, 512, 640, 768, 896, 1280, 1408, 1409)
N_W = 1410
C_ID, C_TRI, C_BLK, C_HM, C_CQ, C_SQ, C_CK, C_SK = 0, 128, 256, 384, 400, 528, 656, 784
N_C = 912


def program(nc, x_in, w_in, c_in, cb_in, krow_in, qrow_in, out):
    with ExitStack() as ctx:
        def sb(name, shape, dt):
            return ctx.enter_context(nc.sbuf_tensor(name, shape, dt))

        def sem(name):
            return ctx.enter_context(nc.semaphore(name))

        ps = ctx.enter_context(nc.psum_tensor("ps", [P, 8, CH], F32))

        kk = sb("kk", [P, H * T], BF16)
        qq = sb("qq", [P, H * T], BF16)
        probs = sb("probs", [P, 3 * 4 * CH], F32)
        x = sb("x", [P, TILES, D], F32)
        vaug = sb("vaug", [P, TILES, H * V1 + VPAD], F32)
        vgrp_area = sb("vgrp_area", [P, 1280], F32)
        vgrp = vgrp_area[:, 0:TILES * (4 * V1 + VPAD)].rearrange("p (t v) -> p t v", t=TILES)
        ot = sb("ot", [P, G * CH], F32)
        att = sb("att", [P, TILES * D], F32)
        w = sb("w", [P, N_W], F32)
        cs = sb("cs", [P, N_C], F32)
        cb = sb("cb", [P, 2 * P], BF16)
        stats = sb("stats", [P, TPC, 6], F32)
        mv = sb("mv", [P, 2, TPC, 2], F32)
        veps = sb("veps", [P, 2, TPC], F32)
        rstd = sb("rstd", [P, 2, TPC], F32)
        neghalf = sb("neghalf", [P, TPC], F32)
        norms = sb("norms", [H, 2, NCH], F32)
        norm2 = sb("norm2", [H, 2], F32)
        bound = sb("bound", [H, 1], F32)
        bound_all = sb("bound_all", [H, 1], F32)
        flag = sb("flag", [1, 1], I32)
        warm = sb("warm", [P, 2], F32)
        negmax = sb("negmax", [P, H * TILES], F32)
        nmt = sb("nmt", [P, 2, 2, P], F32)
        nmp = sb("nmp", [P, 2, PARTS, P], BF16)
        omu = sb("omu", [P, 2], F32)
        rden = sb("rden", [P, 2, 64], F32)
        kvb = sb("kvb", [P, D + H], F32)
        ksum = sb("ksum", [P, 1], F32)

        xt_a = probs[:, 0:T]
        xh_a = probs[:, 2048:3072].rearrange("p (b n) -> p b n", b=2)
        qf = probs[:, 3072:4096].rearrange("p (b n) -> p b n", b=2)
        kf = probs[:, 4096:5120].rearrange("p (b n) -> p b n", b=2)
        res = probs[:, 5120:6144].rearrange("p (b n) -> p b n", b=2)
        sq = vgrp_area[:, 0:2 * CH].rearrange("p (b n) -> p b n", b=2)
        qparts = ot[:, :].bitcast(BF16)[:, 0:2 * PARTS * CH].rearrange("p (b j n) -> p b j n", b=2, j=PARTS)
        kparts = att[:, :].bitcast(BF16)[:, 0:2 * PARTS * CH].rearrange("p (b j n) -> p b j n", b=2, j=PARTS)
        kk32 = kk[:, :].bitcast(F32)
        qq32 = qq[:, :].bitcast(F32)
        area = [kk32[:, T * i:T * (i + 1)] for i in range(8)] + [qq32[:, T * i:T * (i + 1)] for i in range(5)]
        (att_t, xh, prev_r, prev_k, mix_r, mix_k, relu_k, kact, exp_r, one_r, xt_b, q_act, qft) = area
        k_rot, k_exp, k_relu, k_feat = exp_r, one_r, relu_k, kact
        q_rot, q_exp, q_relu, q_feat = prev_r, prev_k, mix_r, mix_k
        heads_out = mix_k
        rot_tmp = q_act
        xt_f = qq32[:, 5 * T:6 * T + 1]
        vb = qq32[:, 6 * T + 8:6 * T + 8 + TILES * (D + 1)].rearrange("p (t n) -> p t n", t=TILES)

        qs = nc.dram_tensor("qs", [PARTS, H, HD, T], BF16, kind="Internal").ap()
        ks = nc.dram_tensor("ks", [PARTS, H, HD, T], BF16, kind="Internal").ap()
        ms = nc.dram_tensor("ms", [2, P, PARTS, P], BF16, kind="Internal").ap()

        def sems(names):
            return [sem(s) for s in names.split()]

        x_loaded = [sem(f"x_loaded{n}") for n in range(NCH)]
        qk_loaded = [sem(f"qk_loaded{n}") for n in range(NCH)]
        w_loaded, c_loaded, rows_loaded, pieces_out, stored = sems("w_loaded c_loaded rows_loaded pieces_out stored")
        pool_ready, dve_step = sems("pool_ready dve_step")
        ln_var, ln_rstd, xh_ready, xt_psum, xt_ready = (
            [sem(f"{s}{i}") for i in range(4)] for s in ("ln_var", "ln_rstd", "xh_ready", "xt_psum", "xt_ready"))
        qkv_psum, qk_sbuf, hi_ready, res_ready, mid_ready, parts_ready, v_ready = sems(
            "qkv_psum qk_sbuf hi_ready res_ready mid_ready parts_ready v_ready")
        norm_psum, norm_ready, squares, bound_ready, all_max, flag_ready, g_scores, g_max, g_turned, g_parts, g_stored, g_rows, g_step = sems(
            "norm_psum norm_ready squares bound_ready all_max flag_ready g_scores g_max g_turned g_parts g_stored g_rows g_step")
        s_done, exp_done, mask_done, pv_done, v_staged, ot_ready, o_turned, o_norm = sems(
            "s_done exp_done mask_done pv_done v_staged ot_ready o_turned o_norm")
        att_psum, att_ready, y_psum, y_added = sems("att_psum att_ready y_psum y_added")
        shifted, mixed, fk_psum, fr_psum, relu_ready, exp_r_ready, one_ready, kact_ready, fv_psum, f_added = sems(
            "shifted mixed fk_psum fr_psum relu_ready exp_r_ready one_ready kact_ready fv_psum f_added")
        bqkv_psum, bv_ready, rot_ready, feat_act, feat_ready, qft_psum, qft_ready, kv_psum, kv_ready = sems(
            "bqkv_psum bv_ready rot_ready feat_act feat_ready qft_psum qft_ready kv_psum kv_ready")
        n_psum, n_ready, nt_psum, nt_ready, y2_psum, y2_added = sems("n_psum n_ready nt_psum nt_ready y2_psum y2_added")

        ident = cs[:, C_ID:C_ID + P]
        block = ctx.enter_context(nc.Block())

        def kbs(c):
            return TPC * (c + 1)

        def kbs_before(c):
            return sum(G * kbs(i) for i in range(c))

        def reuse(c, per_kb, slot):
            return min((per_kb * kbs(i) - 1 - slot) % 3 for i in (c, max(c - 1, 0)))

        def at_least(eng, s, count):
            if count > 0:
                eng.wait_ge(s, count)

        def cols(n):
            return slice(CH * n, CH * (n + 1))

        def tiles(n):
            return slice(TPC * n, TPC * (n + 1))

        def wave(stages):
            last = max(lag for lag, _ in stages)
            for s in range(NCH + last):
                for lag, stage in sorted(stages, key=lambda x: -x[0]):
                    if 0 <= s - lag < NCH:
                        stage(s - lag)

        LN1, LN2, LN3, LN4 = range(4)

        @block.sync
        def _(sp):
            xd = x_in.rearrange("(t p) d -> p t d", p=P)
            for n in range(NCH):
                sp.dma_start(x[:, tiles(n), :], xd[:, tiles(n), :]).then_inc(x_loaded[n], 16)
                if n == 0:
                    sp.dma_start(cs[:, :], c_in).then_inc(c_loaded, 16)
                    sp.dma_start(w[:, :], w_in).then_inc(w_loaded, 16)
            sp.dma_start(cb[:, :], cb_in.bitcast(BF16)).then_inc(rows_loaded, 16)
            sp.dma_start(kk[PAIR_ROWS:ROWS, :], krow_in.bitcast(BF16)).then_inc(rows_loaded, 16)
            sp.dma_start(qq[PAIR_ROWS:ROWS, :], qrow_in.bitcast(BF16)).then_inc(rows_loaded, 16)
            kk3 = kk[:, :].rearrange("p (h t) -> p h t", h=H)
            qq3 = qq[:, :].rearrange("p (h t) -> p h t", h=H)
            for n in range(NCH):
                sp.wait_ge(parts_ready, 2 * (n + 1))
                sp.dma_start(qs.rearrange("j h d t -> (h d) j t")[:, :, cols(n)], qparts[:, n % 2]).then_inc(pieces_out, 16)
                sp.dma_start(ks.rearrange("j h d t -> (h d) j t")[:, :, cols(n)], kparts[:, n % 2]).then_inc(pieces_out, 16)
                sp.wait_ge(pieces_out, 32 * (n + 1))
                for j in range(PARTS):
                    for i in range(PARTS):
                        r = HD * (PARTS * j + i)
                        sp.dma_start(qq3[r:r + HD, :, cols(n)],
                                     qs[j].rearrange("h d t -> d h t")[:, :, cols(n)]).then_inc(qk_loaded[n], 16)
                        sp.dma_start(kk3[r:r + HD, :, cols(n)],
                                     ks[i].rearrange("h d t -> d h t")[:, :, cols(n)]).then_inc(qk_loaded[n], 16)
            sp.wait_ge(flag_ready, 1)
            small = sp.value_load(flag[0:1, 0:1], min_val=0, max_val=1)
            with sp.If(small == 0):
                sp.wait_ge(g_parts, 2)
                sp.dma_start(ms.rearrange("a p j q -> p a (j q)"), nmp[:, :, :, :].rearrange("p a j q -> p a (j q)")).then_inc(g_stored, 16)
                sp.wait_ge(g_stored, 16)
                sp.dma_start(qq[SHIFT_ROW:ROWS, :].rearrange("j (r q) -> j r q", q=P), ms.rearrange("a p j q -> j (a p) q")).then_inc(g_rows, 16)
            od = out.rearrange("(t p) d -> p t d", p=P)
            for n in range(NCH):
                sp.wait_ge(f_added, NCH + n + 1)
                sp.dma_start(od[:, tiles(n), :], x[:, tiles(n), :]).then_inc(stored, 16)
            sp.wait_ge(stored, 16 * NCH)

        @block.gpsimd
        def _(pool):
            nc.gpsimd.memset(neghalf[:], -0.5).then_inc(pool_ready, 1)
            nc.gpsimd.memset(vaug[:], 1.0).then_inc(pool_ready, 1)
            pool.wait_ge(pool_ready, 1)

            def rstd_of(l, n):
                pool.wait_ge(ln_var[l], n + 1)
                nc.gpsimd.tensor_tensor(rstd[:, n % 2], veps[:, n % 2], neghalf[:], ALU.pow).then_inc(ln_rstd[l], 1)

            def middle_parts(n):
                for s, pt in ((0, qparts), (1, kparts)):
                    pool.wait_ge(res_ready, 2 * n + s + 1)
                    nc.gpsimd.tensor_copy(pt[:, n % 2, 1], res[:, s]).then_inc(mid_ready, 1)

            wave([(0, lambda n: rstd_of(LN1, n)), (2, middle_parts)])
            pool.wait_ge(bound_ready, 1)
            nc.gpsimd.partition_all_reduce(bound_all[:], bound[:], H, RMAX).then_inc(all_max, 1)

            def one_plus(f, n):
                pool.wait_ge(exp_r_ready, NCH * f + n + 1)
                nc.gpsimd.tensor_scalar(one_r[:, cols(n)], exp_r[:, cols(n)], 1.0, 1.0, ALU.mult, ALU.add).then_inc(one_ready, 1)

            wave([(1, lambda n: rstd_of(LN2, n)), (4, lambda n: one_plus(0, n)), (5, lambda n: rstd_of(LN3, n))])
            wave([(2, lambda n: rstd_of(LN4, n)), (5, lambda n: one_plus(1, n))])

        @block.scalar
        def _(act):
            act.wait_ge(pool_ready, 1)
            nc.scalar.activation(warm[:, 0:1], neghalf[:, 0:1], ACT.Exp).then_inc(exp_done, 3)

            def turned(psum, ready, n, bank, dst):
                act.wait_ge(psum, n + 1)
                nc.scalar.copy(dst, ps[:, bank, :]).then_inc(ready, 1)

            def take_qk(n):
                act.wait_ge(qkv_psum, n + 1)
                if n >= 2:
                    act.wait_ge(parts_ready, 2 * (n - 1))
                    act.wait_ge(pieces_out, 32 * (n - 1))
                nc.scalar.mul(qf[:, n % 2], ps[:, 4, :], float(HD) ** -0.5).then_inc(qk_sbuf, 1)
                nc.scalar.copy(kf[:, n % 2], ps[:, 5, :]).then_inc(qk_sbuf, 1)
                act.wait_ge(qk_sbuf, 2 * n + 2)
                nc.scalar.copy(qparts[:, n % 2, 0], qf[:, n % 2]).then_inc(hi_ready, 1)
                nc.scalar.copy(kparts[:, n % 2, 0], kf[:, n % 2]).then_inc(hi_ready, 1)
                for s, full in enumerate((qf, kf)):
                    at_least(act, norm_psum, n)
                    nc.scalar.square(sq[:, s], full[:, n % 2]).then_inc(squares, 1)

            wave([(1, lambda n: turned(xt_psum[LN1], xt_ready[LN1], n, 2 + n % 2, xt_a[:, cols(n)])), (2, take_qk)])

            def exps(c, g):
                k0 = g * kbs(c) + kbs_before(c)
                for kb in range(kbs(c)):
                    w0 = max(0, kb - TPC * c) * P
                    slot = probs[:, kb % 3 * 4 * CH:(kb % 3 + 1) * 4 * CH].rearrange("p (h q) -> p h q", h=4)
                    for u in range(2):
                        n = 2 * kb + u
                        if u == 0:
                            act.wait_ge(pv_done, k0 + (kb + 1 if kb >= 3 else 3 - reuse(c, 1, kb)))
                        act.wait_ge(s_done, k0 * 2 + n + 1)
                        nc.scalar.activation(slot[:, 2 * u:2 * u + 2, w0:CH], ps[:, 2 * (n % 3):2 * (n % 3) + 2, w0:CH],
                                             ACT.Exp).then_inc(exp_done, 1)

            for c in range(NCH):
                with act.Fori(0, G) as g:
                    exps(c, g)

            def shift(f, n):
                act.wait_ge(xt_ready[(LN2, LN4)[f]], n + 1)
                nc.scalar.activation(prev_r[:, cols(n)], xt_f[:, cols(n)], ACT.Copy, scale=omu[:, 0:1]).then_inc(shifted, 1)
                nc.scalar.activation(prev_k[:, cols(n)], xt_f[:, cols(n)], ACT.Copy, scale=omu[:, 1:2]).then_inc(shifted, 1)

            def gate(f, n, bank):
                act.wait_ge(fk_psum, NCH * f + n + 1)
                nc.scalar.activation(relu_k[:, cols(n)], ps[:, bank, :], ACT.Relu).then_inc(relu_ready, 1)
                act.wait_ge(fr_psum, NCH * f + n + 1)
                nc.scalar.activation(exp_r[:, cols(n)], ps[:, bank + 1, :], ACT.Exp, scale=-1.0).then_inc(exp_r_ready, 1)

            def take_v(n):
                act.wait_ge(bqkv_psum, n + 1)
                nc.scalar.copy(vb[:, tiles(n), 0:D], ps[:, 4, :].rearrange("p (t d) -> p t d", t=TPC)).then_inc(bv_ready, 1)

            def feature_parts(n):
                for s, (src, e, r) in enumerate(((q_rot, q_exp, q_relu), (k_rot, k_exp, k_relu))):
                    act.wait_ge(rot_ready, 2 * n + s + 1)
                    nc.scalar.activation(e[:, cols(n)], src[:, cols(n)], ACT.Exp).then_inc(feat_act, 1)
                    nc.scalar.activation(r[:, cols(n)], src[:, cols(n)], ACT.Relu).then_inc(feat_act, 1)

            wave([(0, lambda n: turned(att_psum, att_ready, n, 0, att_t[:, cols(n)])),
                  (2, lambda n: turned(xt_psum[LN2], xt_ready[LN2], n, 2, xt_f[:, 1 + CH * n:1 + CH * (n + 1)])),
                  (3, lambda n: shift(0, n)),
                  (4, lambda n: gate(0, n, 3)),
                  (6, lambda n: turned(xt_psum[LN3], xt_ready[LN3], n, 0, xt_b[:, cols(n)])),
                  (7, take_v),
                  (8, feature_parts),
                  (9, lambda n: turned(qft_psum, qft_ready, n, 2, qft[:, cols(n)]))])
            wave([(1, lambda n: turned(nt_psum, nt_ready, n, 2, att_t[:, cols(n)])),
                  (3, lambda n: turned(xt_psum[LN4], xt_ready[LN4], n, 4, xt_f[:, 1 + CH * n:1 + CH * (n + 1)])),
                  (4, lambda n: shift(1, n)),
                  (5, lambda n: gate(1, n, 5))])

        @block.vector
        def _(dve):
            steps = [0]

            def then(ins):
                steps[0] += 1
                ins.then_inc(dve_step, 1)
                dve.wait_ge(dve_step, steps[0])

            def ln_stats(l, n):
                for j in range(TPC):
                    ins = nc.vector.bn_stats(stats[:, j, :], x[:, TPC * n + j, :])
                then(ins)
                for j in range(TPC):
                    ins = nc.vector.bn_aggr(mv[:, n % 2, j, :], stats[:, j, :])
                then(ins)
                nc.vector.tensor_scalar(veps[:, n % 2], mv[:, n % 2, :, 1], EPS, None, ALU.add).then_inc(ln_var[l], 1)

            def ln_apply(l, n, dst):
                dve.wait_ge(ln_rstd[l], n + 1)
                for j in range(TPC):
                    ins = nc.vector.tensor_scalar(dst[:, P * j:P * (j + 1)], x[:, TPC * n + j, :], mv[:, n % 2, j, 0:1],
                                                  rstd[:, n % 2, j:j + 1], ALU.subtract, ALU.mult)
                ins.then_inc(xh_ready[l], 1)

            def ln1_stats(n):
                dve.wait_ge(x_loaded[n], 16)
                ln_stats(LN1, n)

            def ln1_apply(n):
                if n >= 2:
                    dve.wait_ge(xt_psum[LN1], n - 1)
                ln_apply(LN1, n, xh_a[:, n % 2])

            def split(n):
                dve.wait_ge(qkv_psum, n + 1)
                dve.wait_ge(pool_ready, 2)
                nc.vector.tensor_copy(
                    vaug[:, tiles(n), 0:H * V1].rearrange("p t (h v) -> p t h v", h=H)[:, :, :, 0:HD],
                    ps[:, 6, :].rearrange("p (t h v) -> p t h v", t=TPC, h=H)).then_inc(v_ready, 1)
                for s, (full, pt) in enumerate(((qf, qparts), (kf, kparts))):
                    dve.wait_ge(hi_ready, 2 * n + s + 1)
                    if n >= 1:
                        dve.wait_ge(parts_ready, 2 * n - 1 + s)
                        dve.wait_ge(mid_ready, 2 * n - 1 + s)
                    nc.vector.tensor_tensor(res[:, s], full[:, n % 2], pt[:, n % 2, 0], ALU.subtract).then_inc(res_ready, 1)
                for s, pt in enumerate((qparts, kparts)):
                    dve.wait_ge(mid_ready, 2 * n + s + 1)
                    nc.vector.tensor_tensor(pt[:, n % 2, 2], res[:, s], pt[:, n % 2, 1], ALU.subtract).then_inc(parts_ready, 1)

            def norm_max(n):
                dve.wait_ge(norm_psum, n + 1)
                nc.vector.tensor_reduce(norms[:, :, n:n + 1], ps[0:H, 0:2, :], AX.X, ALU.max).then_inc(norm_ready, 1)

            dve.wait_ge(w_loaded, 16)
            nc.vector.tensor_scalar(omu[:, :], w[:, MU_R:MU_K + 1], -1.0, 1.0, ALU.mult, ALU.add)
            wave([(0, ln1_stats), (1, ln1_apply), (2, split), (3, norm_max)])

            dve.wait_ge(norm_ready, NCH)
            then(nc.vector.tensor_reduce(norm2[:, :], norms[:, :, :], AX.X, ALU.max))
            nc.vector.tensor_tensor(bound[:, :], norm2[:, 0:1], norm2[:, 1:2], ALU.mult).then_inc(bound_ready, 1)
            dve.wait_ge(all_max, 1)
            nc.vector.tensor_scalar(flag[0:1, 0:1], bound_all[0:1, 0:1], SHIFT ** 2, None, ALU.is_le).then_inc(flag_ready, 1)
            dve.wait_ge(flag_ready, 1)
            small = dve.value_load(flag[0:1, 0:1], min_val=0, max_val=1)
            with dve.If(small == 0):
                nc.vector.memset(warm[:, 1:2], 0.0).then_inc(g_max, 2)
                for qb in range(TILES):
                    with dve.Fori(0, H // 2) as hp:
                        for i in range(2):
                            dve.wait_ge(g_scores, hp * 2 + (H * qb + i + 1))
                            nq = -(-(qb + 1) * P // CH)
                            nc.vector.tensor_reduce(negmax[:, bass.ds(hp * (2 * TILES) + (i * TILES + qb), 1)],
                                                    ps[:, 4 * i:4 * i + 4, :].rearrange("p b n -> p (b n)")[:, 0:(qb + 1) * P],
                                                    AX.X, ALU.max, negate=True).then_inc(g_max, 1)
                for a in range(2):
                    dve.wait_ge(g_turned, a + 1)
                    n1, n2, n3 = (nmp[:, a, j, :] for j in range(PARTS))
                    full, rest = nmt[:, a, 0, :], nmt[:, a, 1, :]
                    nc.vector.tensor_copy(full, ps[:, a, 0:P]).then_inc(g_step, 1)
                    dve.wait_ge(g_step, 4 * a + 1)
                    nc.vector.tensor_copy(n1, full).then_inc(g_step, 1)
                    dve.wait_ge(g_step, 4 * a + 2)
                    nc.vector.tensor_tensor(rest, full, n1, ALU.subtract).then_inc(g_step, 1)
                    dve.wait_ge(g_step, 4 * a + 3)
                    nc.vector.tensor_copy(n2, rest).then_inc(g_step, 1)
                    dve.wait_ge(g_step, 4 * a + 4)
                    nc.vector.tensor_tensor(n3, rest, n2, ALU.subtract).then_inc(g_parts, 1)

            def group(c, g):
                k0 = g * kbs(c) + kbs_before(c)
                dve.wait_ge(pv_done, k0 + 3)
                src = vaug[:, 0:kbs(c), bass.ds(g * (4 * V1), 4 * V1)]
                nc.vector.tensor_copy(vgrp[:, 0:kbs(c), 0:4 * V1], src).then_inc(v_staged, 1)
                for j in range(TPC):
                    kb = TPC * c + j
                    slot = probs[:, kb % 3 * 4 * CH:(kb % 3 + 1) * 4 * CH].rearrange("p (h q) -> p h q", h=4)[:, :, P * j:P * (j + 1)]
                    dve.wait_ge(exp_done, k0 * 2 + (3 + 2 * (kb + 1)))
                    nc.vector.tensor_tensor(slot, slot, cs[:, C_TRI:C_TRI + P].unsqueeze(1).broadcast_to([P, 4, P]),
                                            ALU.min).then_inc(mask_done, 1)
                dve.wait_ge(pv_done, k0 + (3 + kbs(c)))
                nc.vector.tensor_copy(ot[:, bass.ds(g * CH, CH)], ps[:, 6, :]).then_inc(ot_ready, 1)

            def normalize(c):
                for j in range(TPC):
                    t = TPC * c + j
                    dve.wait_ge(o_turned, t + 1)
                    if t >= 2:
                        dve.wait_ge(o_norm, t - 1)
                    sums = ps[:, 7, :].rearrange("p (h r) -> p h r", h=H)
                    inv = rden[:, j % 2, 0:H]
                    then(nc.vector.reciprocal(inv, sums[:, :, HD]))
                    nc.vector.tensor_tensor(att[:, D * t:D * (t + 1)].rearrange("p (h v) -> p h v", h=H), sums[:, :, 0:HD],
                                            inv.unsqueeze(2).broadcast_to([P, H, HD]), ALU.mult).then_inc(o_norm, 1)

            dve.wait_ge(v_ready, NCH)
            dve.wait_ge(norm_psum, NCH)
            nc.vector.memset(vgrp, 0.0).then_inc(ot_ready, 1)
            dve.wait_ge(ot_ready, 1)
            for c in range(NCH):
                if c:
                    dve.wait_ge(o_turned, TPC * c)
                with dve.Fori(0, G) as g:
                    group(c, g)
                normalize(c)

            nc.vector.memset(vb[:, :, D:D + 1], 1.0)
            nc.vector.memset(xt_f[:, 0:1], 0.0)

            def add_y(n):
                dve.wait_ge(y_psum, n + 1)
                nc.vector.tensor_tensor(x[:, tiles(n), :], ps[:, 1, :].rearrange("p (t d) -> p t d", t=TPC), x[:, tiles(n), :],
                                        ALU.add).then_inc(y_added, 1)
                dve.wait_ge(y_added, n + 1)
                ln_stats(LN2, n)

            def mix(f, n):
                for i, (prev, mixed_t) in enumerate(((prev_r, mix_r), (prev_k, mix_k))):
                    dve.wait_ge(shifted, 2 * (NCH * f + n) + i + 1)
                    nc.vector.scalar_tensor_tensor(mixed_t[:, cols(n)], xt_f[:, 1 + CH * n:1 + CH * (n + 1)],
                                                   w[:, MU_R + i:MU_R + i + 1], prev[:, cols(n)],
                                                   ALU.mult, ALU.add).then_inc(mixed, 1)

            def k_squared(f, n, bank):
                dve.wait_ge(relu_ready, NCH * f + n + 1)
                nc.vector.scalar_tensor_tensor(kact[:, cols(n)], ps[:, bank, :], 0.0, relu_k[:, cols(n)],
                                               ALU.max, ALU.mult).then_inc(kact_ready, 1)

            def add_mix(f, n, bank, l):
                dve.wait_ge(one_ready, NCH * f + n + 1)
                then(nc.vector.reciprocal(exp_r[:, cols(n)], one_r[:, cols(n)]))
                dve.wait_ge(fv_psum, NCH * f + n + 1)
                then(nc.vector.tensor_tensor(exp_r[:, cols(n)], ps[:, bank, :], exp_r[:, cols(n)], ALU.mult))
                nc.vector.tensor_tensor(x[:, tiles(n), :], x[:, tiles(n), :], exp_r[:, cols(n)].rearrange("p (t d) -> p t d", t=TPC),
                                        ALU.add).then_inc(f_added, 1)
                if l is not None:
                    dve.wait_ge(f_added, NCH * f + n + 1)
                    ln_stats(l, n)

            def rope(n):
                dve.wait_ge(bqkv_psum, n + 1)
                for bank, rot, c_cos, c_sin in ((5, q_rot, C_CQ, C_SQ), (7, k_rot, C_CK, C_SK)):
                    a = ps[:, bank, :].rearrange("p (t h e) -> p t h e", t=TPC, h=H)
                    cos, sin = (cs[:, c0 + HD * TPC * n:c0 + HD * TPC * (n + 1)].rearrange("p (t e) -> p t e", t=TPC).unsqueeze(2)
                                for c0 in (c_cos, c_sin))
                    r, tmp = (z[:, cols(n)].rearrange("p (t h e) -> p t h e", t=TPC, h=H) for z in (rot, rot_tmp))
                    e = HD // 2
                    nc.vector.tensor_tensor(r, a, cos.broadcast_to([P, TPC, H, HD]), ALU.mult)
                    nc.vector.tensor_tensor(tmp[:, :, :, 0:e], a[:, :, :, e:], sin[:, :, :, 0:e].broadcast_to([P, TPC, H, e]), ALU.mult)
                    then(nc.vector.tensor_tensor(tmp[:, :, :, e:], a[:, :, :, 0:e], sin[:, :, :, e:].broadcast_to([P, TPC, H, e]), ALU.mult))
                    nc.vector.tensor_tensor(rot[:, cols(n)], rot[:, cols(n)], rot_tmp[:, cols(n)], ALU.add).then_inc(rot_ready, 1)
                    dve.wait_ge(rot_ready, 2 * n + (1 if bank == 5 else 2))

            def features(n):
                for s, (e, r, feat) in enumerate(((q_exp, q_relu, q_feat), (k_exp, k_relu, k_feat))):
                    dve.wait_ge(feat_act, 4 * n + 2 * s + 2)
                    nc.vector.scalar_tensor_tensor(feat[:, cols(n)], e[:, cols(n)], 1.0, r[:, cols(n)],
                                                   ALU.min, ALU.add).then_inc(feat_ready, 1)

            wave([(1, add_y),
                  (2, lambda n: ln_apply(LN2, n, xh[:, cols(n)])),
                  (3, lambda n: mix(0, n)),
                  (4, lambda n: k_squared(0, n, 3)),
                  (5, lambda n: add_mix(0, n, 1, LN3)),
                  (6, lambda n: ln_apply(LN3, n, xh[:, cols(n)])),
                  (7, rope),
                  (8, features)])

            dve.wait_ge(kv_psum, 1)
            nc.vector.tensor_tensor(kvb[:, 0:D], ps[:, 6, 0:D], cs[:, C_BLK:C_BLK + D], ALU.mult)
            nc.vector.tensor_scalar(kvb[:, D:D + H], cs[:, C_HM:C_HM + H], ps[:, 6, D:D + 1], None, ALU.mult).then_inc(kv_ready, 1)

            def divide(n):
                dve.wait_ge(n_psum, n + 1)
                inv = rden[:, n % 2, :]
                then(nc.vector.tensor_scalar(inv, ps[:, 1, 0:TPC * H], 1e-6, None, ALU.max))
                then(nc.vector.reciprocal(inv, inv))
                nc.vector.tensor_tensor(heads_out[:, cols(n)].rearrange("p (h v) -> p h v", v=HD),
                                        ps[:, 0, :].rearrange("p (h v) -> p h v", v=HD),
                                        inv.unsqueeze(2).broadcast_to([P, TPC * H, HD]), ALU.mult).then_inc(n_ready, 1)

            def add_y2(n):
                dve.wait_ge(y2_psum, n + 1)
                nc.vector.tensor_tensor(x[:, tiles(n), :], ps[:, 3, :].rearrange("p (t d) -> p t d", t=TPC), x[:, tiles(n), :],
                                        ALU.add).then_inc(y2_added, 1)
                dve.wait_ge(y2_added, n + 1)
                ln_stats(LN4, n)

            wave([(0, divide),
                  (2, add_y2),
                  (3, lambda n: ln_apply(LN4, n, xh[:, cols(n)])),
                  (4, lambda n: mix(1, n)),
                  (5, lambda n: k_squared(1, n, 5)),
                  (6, lambda n: add_mix(1, n, 7, None))])

        @block.tensor
        def _(pe):
            def turn(src, bank, done):
                for j in range(TPC):
                    ins = nc.tensor.transpose(ps[:, bank, P * j:P * (j + 1)], src[:, P * j:P * (j + 1)], ident)
                ins.then_inc(done, 1)

            def natural(bank, src, c0):
                for j in range(TPC):
                    ins = nc.tensor.matmul(ps[:, bank, P * j:P * (j + 1)], src[:, P * j:P * (j + 1)], w[:, c0:c0 + D],
                                           start=True, stop=True)
                return ins

            def turn_ln1(n):
                pe.wait_ge(xh_ready[LN1], n + 1)
                at_least(pe, xt_ready[LN1], n - 1)
                turn(xh_a[:, n % 2], 2 + n % 2, xt_psum[LN1])

            def qkv(n):
                pe.wait_ge(xt_ready[LN1], n + 1)
                if n:
                    pe.wait_ge(qk_sbuf, 2 * n)
                    pe.wait_ge(v_ready, n)
                src = xt_a[:, cols(n)]
                nc.tensor.matmul(ps[:, 4, :], w[:, W_Q:W_Q + D], src, start=True, stop=True)
                nc.tensor.matmul(ps[:, 5, :], w[:, W_K:W_K + D], src, start=True, stop=True)
                natural(6, src, W_V).then_inc(qkv_psum, 1)

            pe.wait_ge(c_loaded, 16)
            nc.tensor.transpose(ps[:, 7, 0:P], ident, ident).then_inc(pv_done, 3)
            pe.wait_ge(w_loaded, 16)

            def square_norms(n):
                pe.wait_ge(squares, 2 * n + 2)
                at_least(pe, norm_ready, n)
                for s in range(2):
                    ins = nc.tensor.matmul(ps[0:H, s, :], cs[:, C_HM:C_HM + H], sq[:, s], start=True, stop=True)
                ins.then_inc(norm_psum, 1)

            wave([(1, turn_ln1), (2, qkv), (3, square_norms)])

            for n in range(NCH):
                pe.wait_ge(qk_loaded[n], 16 * 2 * PARTS * PARTS)
            pe.wait_ge(rows_loaded, 48)
            pe.wait_ge(flag_ready, 1)
            small = pe.value_load(flag[0:1, 0:1], min_val=0, max_val=1)
            with pe.If(small == 0):
                pe.wait_ge(v_ready, NCH)
                pe.wait_ge(qk_sbuf, 2 * NCH)
                pe.wait_ge(norm_ready, NCH)
                for qb in range(TILES):
                    with pe.Fori(0, H // 2) as hp:
                        for i in range(2):
                            head = hp * (2 * T) + i * T
                            pe.wait_ge(g_max, hp * 2 + (H * qb + i + 1))
                            for k0 in range(0, (qb + 1) * P, CH):
                                k1 = min(k0 + CH, (qb + 1) * P)
                                bank = 4 * i + k0 // CH
                                ins = nc.tensor.matmul(ps[:, bank, 0:k1 - k0], qq[0:SHIFT_ROW, bass.ds(head + qb * P, P)],
                                                       kk[0:SHIFT_ROW, bass.ds(head + k0, k1 - k0)],
                                                       start=True, stop=True)
                            ins = nc.tensor.matmul(ps[:, bank, k1 - k0 - P:k1 - k0], cb[:, 0:P], cb[:, P:2 * P],
                                                   start=False, stop=True, skip_group_check=True)
                            ins.then_inc(g_scores, 1)
                pe.wait_ge(g_max, H * TILES + 2)
                for a in range(2):
                    nc.tensor.transpose(ps[:, a, 0:P], negmax[:, P * a:P * (a + 1)], ident).then_inc(g_turned, 1)
                pe.wait_ge(g_parts, 2)
                pe.wait_ge(g_rows, 16)

            def score(c, g, n):
                kb, u = n // 2, n % 2
                w0 = max(0, kb - TPC * c) * P
                k0 = g * kbs(c) + kbs_before(c)
                b = n % 3
                pe.wait_ge(exp_done, k0 * 2 + (n + 1 if n >= 3 else 3 - reuse(c, 2, n)))
                for i in range(2):
                    head = g * (4 * T) + (2 * u + i) * T
                    ins = nc.tensor.matmul(ps[:, 2 * b + i, w0:CH], kk[0:ROWS, bass.ds(head + kb * P, P)],
                                           qq[0:ROWS, bass.ds(head + (c * CH + w0), CH - w0)], start=True, stop=True)
                ins.then_inc(s_done, 1)

            def weigh(c, g, kb):
                j = kb - TPC * c
                w0 = max(0, j) * P
                k0 = g * kbs(c) + kbs_before(c)
                if kb == 0:
                    pe.wait_ge(v_staged, g + (G * c + 1))
                    pe.wait_ge(ot_ready, g + (G * c + 1))
                pe.wait_ge(exp_done, k0 * 2 + (3 + 2 * (kb + 1)))
                if j >= 0:
                    pe.wait_ge(mask_done, g * TPC + (G * TPC * c + j + 1))
                slot = probs[:, kb % 3 * 4 * CH:(kb % 3 + 1) * 4 * CH].rearrange("p (h q) -> p h q", h=4)
                for i in range(4):
                    ins = nc.tensor.matmul(ps[32 * i:32 * i + 32, 6, w0:CH], vgrp[:, kb, V1 * i:V1 * i + 32], slot[:, i, w0:CH],
                                           start=(kb == 0), stop=(j >= 0), skip_group_check=True)
                ins.then_inc(pv_done, 1)

            def group(c, g, nxt):
                for kb in range(1, kbs(c)):
                    score(c, g, 2 * kb)
                    score(c, g, 2 * kb + 1)
                    weigh(c, g, kb - 1)
                if nxt is not None:
                    score(*nxt, 0)
                    score(*nxt, 1)
                weigh(c, g, kbs(c) - 1)

            def turn_sums(c):
                pe.wait_ge(ot_ready, G * (c + 1) + 1)
                for j in range(TPC):
                    t = TPC * c + j
                    at_least(pe, o_norm, t)
                    for g in range(G):
                        ins = nc.tensor.transpose(ps[:, 7, P * g:P * (g + 1)], ot[:, g * CH + j * P:g * CH + (j + 1) * P], ident)
                    ins.then_inc(o_turned, 1)

            pe.wait_ge(v_ready, NCH)
            pe.wait_ge(norm_ready, NCH)
            pe.wait_ge(qk_sbuf, 2 * NCH)
            score(0, 0, 0)
            score(0, 0, 1)
            for c in range(NCH):
                with pe.Fori(0, G - 1) as g:
                    group(c, g, (c, g + 1))
                group(c, G - 1, (c + 1, 0) if c + 1 < NCH else None)
                turn_sums(c)

            def turn_att(n):
                pe.wait_ge(o_norm, TPC * (n + 1))
                at_least(pe, att_ready, n)
                turn(att[:, cols(n)], 0, att_psum)

            def project(n):
                pe.wait_ge(att_ready, n + 1)
                at_least(pe, y_added, n)
                natural(1, att_t[:, cols(n)], W_O).then_inc(y_psum, 1)

            def turn_xh(l, n, bank):
                pe.wait_ge(xh_ready[l], n + 1)
                at_least(pe, xt_ready[l], n)
                turn(xh[:, cols(n)], bank, xt_psum[l])

            def mix_in(f, n, bank):
                pe.wait_ge(mixed, 2 * (NCH * f + n) + 2)
                at_least(pe, kact_ready, NCH * f + n)
                nc.tensor.matmul(ps[:, bank, :], w[:, W_KK:W_KK + D], mix_k[:, cols(n)], start=True, stop=True).then_inc(fk_psum, 1)
                at_least(pe, exp_r_ready, NCH * f + n)
                natural(bank + 1, mix_r[:, cols(n)], W_R).then_inc(fr_psum, 1)

            def mix_out(f, n, bank):
                pe.wait_ge(kact_ready, NCH * f + n + 1)
                at_least(pe, f_added, NCH * f + n)
                natural(bank, kact[:, cols(n)], W_VV).then_inc(fv_psum, 1)

            def mix_in_1(n):
                at_least(pe, bv_ready, n - 2)
                mix_in(0, n, 3)

            def mix_out_1(n):
                pe.wait_ge(y_added, NCH)
                mix_out(0, n, 1)

            def turn_b(n):
                pe.wait_ge(att_ready, NCH)
                turn_xh(LN3, n, 0)

            def qkv_b(n):
                pe.wait_ge(xt_ready[LN3], n + 1)
                at_least(pe, rot_ready, 2 * n)
                pe.wait_ge(exp_r_ready, min(NCH, n + 3))
                at_least(pe, bv_ready, n)
                for i, bank in enumerate((5, 7, 4)):
                    ins = natural(bank, xt_b[:, cols(n)], W_QKV + D * i)
                ins.then_inc(bqkv_psum, 1)

            def summarize(n):
                pe.wait_ge(feat_ready, 2 * n + 1)
                pe.wait_ge(xt_ready[LN2], NCH)
                at_least(pe, qft_ready, n)
                turn(q_feat[:, cols(n)], 2, qft_psum)
                pe.wait_ge(feat_ready, 2 * n + 2)
                pe.wait_ge(bv_ready, n + 1)
                for j in range(TPC):
                    t = TPC * n + j
                    ins = nc.tensor.matmul(ps[:, 6, 0:D + 1], k_feat[:, P * t:P * (t + 1)], vb[:, t, :],
                                           start=(t == 0), stop=(t == TILES - 1))
                if n == NCH - 1:
                    ins.then_inc(kv_psum, 1)

            wave([(0, turn_att), (1, project), (2, lambda n: turn_xh(LN2, n, 2)), (4, mix_in_1), (5, mix_out_1),
                  (6, turn_b), (7, qkv_b), (9, summarize)])

            def numerators(n):
                pe.wait_ge(kv_ready, 1)
                pe.wait_ge(qft_ready, n + 1)
                at_least(pe, n_ready, n)
                for j in range(TPC):
                    t = TPC * n + j
                    q = qft[:, P * t:P * (t + 1)]
                    nc.tensor.matmul(ps[:, 0, P * j:P * (j + 1)], q, kvb[:, 0:D], start=True, stop=True)
                    ins = nc.tensor.matmul(ps[:, 1, H * j:H * (j + 1)], q, kvb[:, D:D + H], start=True, stop=True)
                ins.then_inc(n_psum, 1)

            def turn_heads(n):
                pe.wait_ge(n_ready, n + 1)
                pe.wait_ge(qft_ready, NCH)
                at_least(pe, nt_ready, n)
                turn(heads_out[:, cols(n)], 2, nt_psum)

            def project_b(n):
                pe.wait_ge(nt_ready, n + 1)
                at_least(pe, y2_added, n)
                natural(3, att_t[:, cols(n)], W_OUT).then_inc(y2_psum, 1)

            wave([(0, numerators), (1, turn_heads), (2, project_b), (3, lambda n: turn_xh(LN4, n, 4)),
                  (5, lambda n: mix_in(1, n, 5)), (6, lambda n: mix_out(1, n, 7))])


def constants():
    f = np.float32

    def high(a):
        return (np.ascontiguousarray(a, f).view(np.uint32) & np.uint32(0xFFFF0000)).view(f)

    def bits(a):
        return (np.ascontiguousarray(a, f).view(np.uint32) >> np.uint32(16)).astype(np.uint16)

    c = np.zeros((P, N_C), f)
    c[:, C_ID:C_ID + P] = np.eye(P)
    k, q = np.arange(P)[:, None], np.arange(P)[None, :]
    c[:, C_TRI:C_TRI + P] = np.where(k <= q, f(3e38), f(0))
    c[:, C_BLK:C_BLK + P] = k // HD == q // HD
    c[:, C_HM:C_HM + H] = k // HD == np.arange(H)[None, :]
    inv = (1.0 / f(10000.0) ** (np.arange(0, HD, 2, dtype=f) / f(HD))).astype(f)
    ang = np.arange(T, dtype=f)[:, None] * inv[None, :]
    cos, sin = np.cos(ang), np.sin(ang)
    cos, sin = np.concatenate([cos, cos], 1), np.concatenate([-sin, sin], 1)
    for base, tab, s in ((C_CQ, cos, HD ** -0.5), (C_SQ, sin, HD ** -0.5), (C_CK, cos, 1.0), (C_SK, sin, 1.0)):
        c[:, base:base + TILES * HD] = (tab * f(s)).reshape(TILES, P, HD).transpose(1, 0, 2).reshape(P, -1)
    cb = np.zeros((P, 2 * P), f)
    cb[:, 0:P] = np.eye(P)
    cb[:, P:] = np.where(q > k, -1e30, 0.0)
    slopes = (f(1.0) / f(256.0) ** ((np.arange(H, dtype=f) + f(1)) / f(H))).astype(f)
    parts, rest = [], slopes
    for _ in range(PARTS):
        part = high(rest)
        parts.append(part)
        rest = rest - part
    pos = np.arange(T)
    hi, lo = pos // P * P, pos % P
    krows, qrows = np.zeros((CONST_ROWS, H, T), f), np.zeros((CONST_ROWS, H, T), f)
    for j, part in enumerate(parts):
        r = 4 * j
        krows[r], qrows[r] = hi[None, :], part[:, None]
        krows[r + 1], qrows[r + 1] = part[:, None], -hi[None, :]
        krows[r + 2], qrows[r + 2] = lo[None, :], part[:, None]
        krows[r + 3], qrows[r + 3] = part[:, None], -lo[None, :]
    krows[SHIFT_ROW - PAIR_ROWS:] = 1.0
    qrows[SHIFT_ROW - PAIR_ROWS] = -SHIFT
    return c, bits(cb), bits(krows.reshape(CONST_ROWS, H * T)), bits(qrows.reshape(CONST_ROWS, H * T))


def kernel(L0_attn_a_x, L0_attn_a_W_Q, L0_attn_a_W_K, L0_attn_a_W_V, L0_attn_a_W_O, L0_attn_b_w_qkv, L0_attn_b_w_out,
           L0_ffn_W_r, L0_ffn_W_k, L0_ffn_W_v, L0_ffn_mu_r, L0_ffn_mu_k):
    import concourse.bacc as bacc
    from concourse.bass_utils import run_bass_kernel_spmd

    nc = bacc.Bacc("TRN2", target_bir_lowering=False, num_devices=1)
    weights = np.concatenate(
        [np.asarray(m).T for m in (L0_attn_a_W_Q, L0_attn_a_W_K, L0_attn_a_W_V, L0_attn_a_W_O, L0_ffn_W_r, L0_ffn_W_k,
                                   L0_ffn_W_v, L0_attn_b_w_qkv, L0_attn_b_w_out)]
        + [np.asarray(L0_ffn_mu_r)[:, None], np.asarray(L0_ffn_mu_k)[:, None]], axis=1)
    consts, consts_b, krows, qrows = constants()
    arrays = {
        "in_x": np.ascontiguousarray(np.asarray(L0_attn_a_x).reshape(T, D)),
        "in_weights": np.ascontiguousarray(weights),
        "in_consts": consts, "in_consts_b": consts_b, "in_krows": krows, "in_qrows": qrows,
    }
    args = [nc.dram_tensor(name, a.shape, mybir.dt.from_np(a.dtype), kind="ExternalInput").ap() for name, a in arrays.items()]
    out = nc.dram_tensor("out_y", (T, D), F32, kind="ExternalOutput").ap()
    program(nc, *args, out)
    r = run_bass_kernel_spmd(nc, [arrays], core_ids=[0])
    return r.results[0]["out_y"].reshape(1, T, D)
```

```python
from contextlib import ExitStack

import numpy as np

import concourse.bass as bass
from concourse import mybir

F32 = mybir.dt.float32
BF16 = mybir.dt.bfloat16
I32 = mybir.dt.int32
ALU = mybir.AluOpType
ACT = mybir.ActivationFunctionType
AX = mybir.AxisListType
RMAX = bass.bass_isa.ReduceOp.max

P = 128
T = 2048
D = 128
H = 16
HD = D // H
TILES = T // P
CH = 512
NCH = T // CH
TPC = CH // P
G = H // 4
EPS = 1e-5
PARTS = 3
PAIR_ROWS = PARTS * PARTS * HD
POS_ROWS = 12
SHIFT_ROW = 96
ROWS = SHIFT_ROW + PARTS
CONST_ROWS = ROWS - PAIR_ROWS
SHIFT = 32.0
BOUND = 30.0
V1 = HD + 1
WARM_UP = 2

W_Q, W_K, W_V, W_O, W_R, W_KK, W_VV, W_QKV, W_OUT, MU_R, MU_K = (
    0, 128, 256, 384, 512, 640, 768, 896, 1280, 1408, 1409)
N_W = 1410
C_ID, C_TRI, C_BLK, C_HM, C_CQ, C_SQ, C_CK, C_SK = 0, 128, 256, 384, 400, 528, 656, 784
N_C = 912
B_ID, B_TRI, B_HN = 0, 128, 256
N_B = 288


def program(nc, x_in, w_in, c_in, cb_in, krow_in, qrow_in, out):
    with ExitStack() as ctx:
        def sb(name, shape, dt):
            return ctx.enter_context(nc.sbuf_tensor(name, shape, dt))

        def sem(name):
            return ctx.enter_context(nc.semaphore(name))

        ps = ctx.enter_context(nc.psum_tensor("ps", [P, 8, CH], F32))

        kk = sb("kk", [P, H * T], BF16)
        qq = sb("qq", [P, H * T], BF16)
        probs = sb("probs", [P, 3 * 4 * CH], F32)
        x = sb("x", [P, TILES, D], F32)
        vaug = sb("vaug", [P, TILES, H * V1], F32)
        vgrp_area = sb("vgrp_area", [P, 2 * CH], F32)
        vgrp = vgrp_area[:, 0:TILES * 4 * V1].rearrange("p (t v) -> p t v", t=TILES)
        ot = sb("ot", [P, CH], F32)
        o_inv = sb("o_inv", [P, 4 * TPC], F32)
        att = sb("att", [P, (1 + NCH * G) * TPC * 4 * HD], F32)
        w = sb("w", [P, N_W], F32)
        cs = sb("cs", [P, N_C], F32)
        cb = sb("cb", [P, N_B], BF16)
        stats = sb("stats", [P, NCH, TPC, 6], F32)
        mv = sb("mv", [P, NCH, TPC, 2], F32)
        veps = sb("veps", [P, NCH, TPC], F32)
        rstd = sb("rstd", [P, NCH, TPC], F32)
        negmean = sb("negmean", [P, NCH, TPC], F32)
        shift_by = sb("shift_by", [P, NCH, TPC], F32)
        neghalf = sb("neghalf", [P, TPC], F32)
        norms = sb("norms", [P, 2], F32)
        norms_all = sb("norms_all", [P, 2], F32)
        flag = sb("flag", [1, 1], I32)
        warm = sb("warm", [P, 2], F32)
        negmax = sb("negmax", [P, H * TILES], F32)
        nmp = sb("nmp", [P, 2, PARTS, P], BF16)
        omu = sb("omu", [P, 2], F32)
        rden = sb("rden", [P, TILES * H], F32)

        xt_a = probs[:, 0:T]
        xh_a = probs[:, T:2 * T]
        res = probs[:, 2 * T:3 * T].rearrange("p (b s n) -> p b s n", b=2, s=2)
        sq = vgrp_area[:, 0:2 * CH].bitcast(BF16).rearrange("p (b s n) -> p b s n", b=2, s=2)
        qparts, kparts = (a[:, H * CH * (NCH - 1):][:, 0:NCH * PARTS * CH].rearrange("p (n j t) -> p n j t", n=NCH, j=PARTS)
                          for a in (qq, kk))
        kk32 = kk[:, :].bitcast(F32)
        qq32 = qq[:, :].bitcast(F32)
        area = [kk32[:, T * i:T * (i + 1)] for i in range(8)] + [qq32[:, T * i:T * (i + 1)] for i in range(5)]
        (att_t, xh, prev_r, prev_k, mix_rt, mix_k, relu_k, kact, gate_r, spare, xt_b, q_tmp, qft) = area
        k_rot, k_exp, k_relu, k_feat = gate_r, spare, relu_k, kact
        q_rot, q_exp, q_relu, q_feat = prev_r, prev_k, mix_rt, mix_k
        heads_out = mix_k
        k_tmp = att_t
        xt_f = qq32[:, 5 * T:6 * T + 1]
        vb = qq32[:, 6 * T + 8:6 * T + 8 + TILES * (D + 1)].rearrange("p (t n) -> p t n", t=TILES)
        kvb = qq32[:, 7 * T + CH:7 * T + CH + D + H]
        w_mu = qq32[:, 7 * T + 2 * CH:7 * T + 2 * CH + 2 * D].rearrange("p (i n) -> p i n", i=2)
        nmt = probs[:, 0:4 * P].rearrange("p (a b q) -> p a b q", a=2, b=2)

        qs = nc.dram_tensor("qs", [NCH, PARTS, HD, H, CH], BF16, kind="Internal").ap()
        ks = nc.dram_tensor("ks", [NCH, PARTS, HD, H, CH], BF16, kind="Internal").ap()
        ms = nc.dram_tensor("ms", [2, P, PARTS, P], BF16, kind="Internal").ap()

        def sems(names):
            return [sem(s) for s in names.split()]

        x_loaded = [sem(f"x_loaded{n}") for n in range(NCH)]
        x_again = [sem(f"x_again{n}") for n in range(NCH)]
        qk_loaded = [sem(f"qk_loaded{n}") for n in range(NCH)]
        w_loaded, c_loaded, cb_loaded, rows_loaded, stored = sems("w_loaded c_loaded cb_loaded rows_loaded stored")
        parts_out = [sem(f"parts_out{n}") for n in range(NCH)]
        ln1_ready = [sem(f"ln1_ready{n}") for n in range(NCH)]
        pool_ready, dve_step = sems("pool_ready dve_step")
        ln_var, ln_rstd, ln_shift, xh_ready, xt_psum, xt_ready = (
            [sem(f"{s}{i}") for i in range(4)] for s in ("ln_var", "ln_rstd", "ln_shift", "xh_ready", "xt_psum", "xt_ready"))
        qkv_psum, hi_ready, res_ready, mid_ready, parts_ready, v_ready = sems(
            "qkv_psum hi_ready res_ready mid_ready parts_ready v_ready")
        norm_psum, squares, bound_ready, all_max, flag_ready, g_scores, g_max, g_turned, g_parts, g_stored, g_rows, g_step = sems(
            "norm_psum squares bound_ready all_max flag_ready g_scores g_max g_turned g_parts g_stored g_rows g_step")
        s_done, exp_done, mask_done, pv_done, v_staged, ot_ready, o_turned, o_recip, o_norm = sems(
            "s_done exp_done mask_done pv_done v_staged ot_ready o_turned o_recip o_norm")
        att_psum, att_ready, y_psum, y_added = sems("att_psum att_ready y_psum y_added")
        mu_ready, shifted, mixed, fk_psum, fr_psum, relu_ready, gate_ready, kact_ready, fv_psum, f_added = sems(
            "mu_ready shifted mixed fk_psum fr_psum relu_ready gate_ready kact_ready fv_psum f_added")
        bq_psum, bk_psum, bv_psum, rot_parts_q, rot_parts_k, bv_ready, rot_ready, feat_act, feat_ready, qft_psum, qft_ready, kv_psum, kv_ready = sems(
            "bq_psum bk_psum bv_psum rot_parts_q rot_parts_k bv_ready rot_ready feat_act feat_ready qft_psum qft_ready kv_psum kv_ready")
        n_psum, n_ready, nt_psum, nt_ready, y2_psum, y2_added = sems("n_psum n_ready nt_psum nt_ready y2_psum y2_added")

        ident = cs[:, C_ID:C_ID + P]
        block = ctx.enter_context(nc.Block())

        def kbs(c):
            return TPC * (c + 1)

        def kbs_before(c):
            return sum(G * kbs(i) for i in range(c))

        def score_buffer(c, n):
            return 1 if n == 2 * kbs(c) - 1 and n % 3 == 0 else n % 3

        def back(c, n):
            b = score_buffer(c, n)
            here = [n - m for m in range(n) if score_buffer(c, m) == b]
            before = [n + 2 * kbs(i) - m for i in (c, max(c - 1, 0)) for m in range(2 * kbs(i)) if score_buffer(i, m) == b]
            return min(here or before)

        def probs_slot(i):
            if i % 4 == 1:
                return x[:, :, :].rearrange("p t d -> p (t d)").rearrange("p (h q) -> p h q", h=4)
            k = (0, 0, 1, 2)[i % 4]
            return probs[:, k * 4 * CH:(k + 1) * 4 * CH].rearrange("p (h q) -> p h q", h=4)

        def at_least(eng, s, count):
            if count > 0:
                eng.wait_ge(s, count)

        def cols(n):
            return slice(CH * n, CH * (n + 1))

        def tiles(n):
            return slice(TPC * n, TPC * (n + 1))

        def ln_apply(engine, waits, l, n, dst):
            waits.wait_ge(ln_rstd[l], n + 1)
            for j in range(TPC):
                ins = engine.tensor_scalar(dst[:, P * j:P * (j + 1)], x[:, TPC * n + j, :], negmean[:, n, j:j + 1],
                                           rstd[:, n, j:j + 1], ALU.add, ALU.mult)
            ins.then_inc(xh_ready[l] if l != LN1 else ln1_ready[n], 1)

        def each(*stages):
            for stage in stages:
                for n in range(NCH):
                    stage(n)

        def trail(first, second):
            for n in range(NCH + 1):
                if n < NCH:
                    first(n)
                if n:
                    second(n - 1)

        def low(n):
            return n

        def high(n):
            return 4 + n

        def key_blocks(c):
            full = [(kb, 0) for kb in range(TPC * c)]
            diagonal = [(TPC * c + j, P * j) for j in range(TPC)]
            if not full:
                return diagonal
            order = [b for pair in zip(full[:TPC - 1], diagonal) for b in pair]
            return order + diagonal[TPC - 1:] + full[TPC - 1:]

        def first_part(c):
            return 2 * TPC - 1 if c else TPC // 2

        def runs(c, part):
            if c == 0:
                return [[(0, 2)], [(2, 4)]][part]
            return [[(0, TPC - 1), (TPC * c, TPC * (c + 1))], [(TPC - 1, TPC * c)]][part]

        LN1, LN2, LN3, LN4 = range(4)
        QK_LOADS = 16 * (PARTS + 1 + 2)

        @block.sync
        def _(sp):
            xd = x_in.rearrange("(t p) d -> p t d", p=P)
            for n in range(NCH):
                sp.dma_start(x[:, tiles(n), :], xd[:, tiles(n), :]).then_inc(x_loaded[n], 16)
                if n == 0:
                    sp.dma_start(cs[:, :], c_in).then_inc(c_loaded, 16)
                if n == 1:
                    sp.dma_start(w[:, :], w_in).then_inc(w_loaded, 16)
            sp.dma_start(cb[:, :], cb_in.bitcast(BF16)).then_inc(cb_loaded, 16)
            block_cols = H * CH

            def constant_rows(n):
                a, b = block_cols * n, block_cols * (n + 1)
                sp.dma_start(kk[PAIR_ROWS:ROWS, a:b], krow_in.bitcast(BF16)[:, a:b]).then_inc(qk_loaded[n], 16)
                sp.dma_start(qq[PAIR_ROWS:ROWS, a:b], qrow_in.bitcast(BF16)[:, a:b]).then_inc(qk_loaded[n], 16)

            def parts_to_dram(n):
                sp.wait_ge(parts_ready, 2 * (n + 1))
                sp.dma_start(qs[n].rearrange("j d h t -> (d h) j t"), qparts[:, n]).then_inc(parts_out[n], 16)
                sp.dma_start(ks[n].rearrange("j d h t -> (d h) j t"), kparts[:, n]).then_inc(parts_out[n], 16)

            def rows_from_dram(n):
                sp.wait_ge(parts_out[n], 32)
                a, b = block_cols * n, block_cols * (n + 1)
                q_part = qs[n].rearrange("j d h t -> (j d) (h t)").unsqueeze(0).broadcast_to([PARTS, PARTS * HD, block_cols])
                sp.dma_start(qq[0:PAIR_ROWS, a:b], q_part).then_inc(qk_loaded[n], 16)
                for i in range(PARTS):
                    r = PARTS * HD * i
                    k_part = ks[n, i].rearrange("d h t -> d (h t)").unsqueeze(0).broadcast_to([PARTS, HD, block_cols])
                    sp.dma_start(kk[r:r + PARTS * HD, a:b], k_part).then_inc(qk_loaded[n], 16)

            for n in range(NCH - 1):
                constant_rows(n)
            parts_to_dram(0)
            rows_from_dram(0)
            for n in range(1, NCH):
                parts_to_dram(n)
            for n in range(1, NCH):
                rows_from_dram(n)
            constant_rows(NCH - 1)
            sp.wait_ge(flag_ready, 1)
            small = sp.value_load(flag[0:1, 0:1], min_val=0, max_val=1)
            with sp.If(small == 0):
                sp.wait_ge(g_parts, 2)
                sp.dma_start(ms.rearrange("a p j q -> p a (j q)"), nmp[:, :, :, :].rearrange("p a j q -> p a (j q)")).then_inc(g_stored, 16)
                sp.wait_ge(g_stored, 16)
                sp.dma_start(qq[SHIFT_ROW:ROWS, :].rearrange("j (r q) -> j r q", q=P), ms.rearrange("a p j q -> j (a p) q")).then_inc(g_rows, 16)
            sp.wait_ge(pv_done, 4 + kbs_before(NCH) - 2)
            for n in range(NCH):
                sp.dma_start(x[:, tiles(n), :], xd[:, tiles(n), :]).then_inc(x_again[n], 16)
            od = out.rearrange("(t p) d -> p t d", p=P)
            for n in range(NCH):
                sp.wait_ge(f_added, NCH + n + 1)
                sp.dma_start(od[:, tiles(n), :], x[:, tiles(n), :]).then_inc(stored, 16)
            sp.wait_ge(stored, 16 * NCH)

        @block.gpsimd
        def _(pool):
            nc.gpsimd.memset(neghalf[:], -0.5).then_inc(pool_ready, 1)
            nc.gpsimd.memset(vaug[:], 1.0).then_inc(pool_ready, 1)
            pool.wait_ge(pool_ready, 1)

            def rstd_of(l, n):
                pool.wait_ge(ln_var[l], n + 1)
                nc.gpsimd.tensor_tensor(rstd[:, n], veps[:, n], neghalf[:], ALU.pow).then_inc(ln_rstd[l], 1)

            def shift_of(l, n):
                rstd_of(l, n)
                pool.wait_ge(ln_rstd[l], n + 1)
                nc.gpsimd.tensor_tensor(shift_by[:, n], negmean[:, n], rstd[:, n], ALU.mult).then_inc(ln_shift[l], 1)

            def turned_qk(n):
                for s, (a, b) in enumerate(((q_rot, q_tmp), (k_rot, k_tmp))):
                    pool.wait_ge((rot_parts_q, rot_parts_k)[s], n + 1)
                    nc.gpsimd.tensor_tensor(a[:, cols(n)], a[:, cols(n)], b[:, cols(n)], ALU.add).then_inc(rot_ready, 1)

            def middle_parts(n):
                for s, pt in ((0, qparts), (1, kparts)):
                    pool.wait_ge(res_ready, 2 * n + s + 1)
                    nc.gpsimd.tensor_scalar(pt[:, n, 1], res[:, n % 2, s], 1.0, 0.0, ALU.mult, ALU.add).then_inc(mid_ready, 1)

            for n in range(NCH):
                rstd_of(LN1, n)
                if n % 2:
                    ln_apply(nc.gpsimd, pool, LN1, n, xh_a[:, cols(n)])
            each(middle_parts)
            pool.wait_ge(bound_ready, 1)
            nc.gpsimd.partition_all_reduce(norms_all[:], norms[:], P, RMAX).then_inc(all_max, 1)

            each(lambda n: shift_of(LN2, n))
            each(lambda n: shift_of(LN3, n))
            each(turned_qk)
            each(lambda n: shift_of(LN4, n))

        @block.scalar
        def _(act):
            act.wait_ge(pool_ready, 1)
            nc.scalar.activation(warm[:, 0:1], neghalf[:, 0:1], ACT.Exp).then_inc(exp_done, 3)

            def turned(psum, ready, n, bank, dst):
                act.wait_ge(psum, n + 1)
                nc.scalar.copy(dst, ps[:, bank, :]).then_inc(ready, 1)

            def take_qkv(n):
                at_least(act, norm_psum, n - 1)
                for s, (pt, scale) in enumerate(((qparts, float(HD) ** -0.5), (kparts, 1.0))):
                    b = 4 + 2 * s + n % 2
                    act.wait_ge(qkv_psum, 3 * n + s + 1)
                    nc.scalar.activation(pt[:, n, 0], ps[:, b, :], ACT.Copy, scale=scale)
                    nc.scalar.activation(sq[:, n % 2, s], ps[:, b, :], ACT.Square, scale=scale).then_inc(hi_ready, 1)
                act.wait_ge(qkv_psum, 3 * n + 3)
                act.wait_ge(pool_ready, 2)
                nc.scalar.copy(vaug[:, tiles(n), 0:H * V1].rearrange("p t (h v) -> p t h v", h=H)[:, :, :, 0:HD],
                               ps[:, 1, :].rearrange("p (t h v) -> p t h v", t=TPC, h=H)).then_inc(v_ready, 1)

            def take_xt(n):
                turned(xt_psum[LN1], xt_ready[LN1], n, 0, xt_a[:, cols(n)])

            trail(take_xt, take_qkv)

            def exps(c, g):
                k0 = g * kbs(c) + kbs_before(c)
                for i, (kb, w0) in enumerate(key_blocks(c)):
                    slot = probs_slot(i)
                    for u in range(2):
                        n = 2 * i + u
                        if u == 0:
                            act.wait_ge(pv_done, k0 + (i + 1))
                        act.wait_ge(s_done, k0 * 2 + n + 1)
                        b = 2 * score_buffer(c, n)
                        nc.scalar.activation(slot[:, 2 * u:2 * u + 2, w0:CH], ps[:, b:b + 2, w0:CH],
                                             ACT.Exp).then_inc(exp_done, 1)

            for c in range(NCH):
                with act.Fori(0, G) as g:
                    exps(c, g)

            def ln_act(l, n):
                act.wait_ge(ln_shift[l], n + 1)
                for j in range(TPC):
                    t = TPC * n + j
                    ins = nc.scalar.activation(xh[:, P * t:P * (t + 1)], x[:, t, :], ACT.Identity,
                                               bias=shift_by[:, n, j:j + 1], scale=rstd[:, n, j:j + 1])
                ins.then_inc(xh_ready[l], 1)

            def shift(f, n):
                nc.scalar.activation(prev_r[:, cols(n)], xt_f[:, cols(n)], ACT.Copy, scale=omu[:, 0:1]).then_inc(shifted, 1)

            def load_table(f):
                nc.scalar.activation(warm[:, 0:1], neghalf[:, 0:1], f)

            def relu(f, n):
                act.wait_ge(fk_psum, NCH * f + n + 1)
                nc.scalar.activation(relu_k[:, cols(n)], ps[:, high(n), :], ACT.Relu).then_inc(relu_ready, 1)

            def gate(f, n):
                act.wait_ge(fr_psum, NCH * f + n + 1)
                nc.scalar.activation(gate_r[:, cols(n)], ps[:, low(n), :], ACT.Sigmoid).then_inc(gate_ready, 1)

            def take_v(n):
                act.wait_ge(bv_psum, n + 1)
                nc.scalar.copy(vb[:, tiles(n), 0:D], ps[:, high(n), :].rearrange("p (t d) -> p t d", t=TPC)).then_inc(bv_ready, 1)

            def feature_parts(s, n):
                src, e, r = ((q_rot, q_exp, q_relu), (k_rot, k_exp, k_relu))[s]
                act.wait_ge(rot_ready, 2 * n + s + 1)
                nc.scalar.activation(e[:, cols(n)], src[:, cols(n)], ACT.Exp).then_inc(feat_act, 1)
                nc.scalar.activation(r[:, cols(n)], src[:, cols(n)], ACT.Relu).then_inc(feat_act, 1)

            def turned_f(f, n):
                l = (LN2, LN4)[f]
                turned(xt_psum[l], xt_ready[l], n, low(n), xt_f[:, 1 + CH * n:1 + CH * (n + 1)])
                act.wait_ge(xt_ready[l], n + 1)
                shift(f, n)

            each(lambda n: turned(att_psum, att_ready, n, low(n), att_t[:, cols(n)]))
            trail(lambda n: ln_act(LN2, n),
                  lambda n: turned_f(0, n))
            load_table(ACT.Sigmoid)
            each(lambda n: relu(0, n),
                 lambda n: gate(0, n))
            trail(lambda n: ln_act(LN3, n),
                  lambda n: turned(xt_psum[LN3], xt_ready[LN3], n, low(n), xt_b[:, cols(n)]))
            load_table(ACT.Exp)
            for n in range(NCH):
                take_v(n)
                for s in range(2):
                    feature_parts(s, n)
            each(lambda n: turned(qft_psum, qft_ready, n, low(n), qft[:, cols(n)]),
                 lambda n: turned(nt_psum, nt_ready, n, low(n), att_t[:, cols(n)]))
            trail(lambda n: ln_act(LN4, n),
                  lambda n: turned_f(1, n))
            load_table(ACT.Sigmoid)
            each(lambda n: relu(1, n),
                 lambda n: gate(1, n))

        @block.vector
        def _(dve):
            steps = [0]

            def then(ins):
                steps[0] += 1
                ins.then_inc(dve_step, 1)
                dve.wait_ge(dve_step, steps[0])

            def ln_stats(l, n):
                for j in range(TPC):
                    ins = nc.vector.bn_stats(stats[:, n, j, :], x[:, TPC * n + j, :])
                then(ins)
                for j in range(TPC):
                    ins = nc.vector.bn_aggr(mv[:, n, j, :], stats[:, n, j, :])
                then(ins)
                nc.vector.tensor_scalar(negmean[:, n], mv[:, n, :, 0], -1.0, None, ALU.mult)
                nc.vector.tensor_scalar(veps[:, n], mv[:, n, :, 1], EPS, None, ALU.add).then_inc(ln_var[l], 1)

            def ln1_stats(n):
                dve.wait_ge(x_loaded[n], 16)
                ln_stats(LN1, n)

            def ln1_apply(n):
                if n % 2 == 0:
                    ln_apply(nc.vector, dve, LN1, n, xh_a[:, cols(n)])

            def split(n):
                for s, (pt, scale) in enumerate(((qparts, float(HD) ** -0.5), (kparts, 1.0))):
                    dve.wait_ge(hi_ready, 2 * n + s + 1)
                    if n >= 2:
                        dve.wait_ge(parts_ready, 2 * (n - 2) + s + 1)
                        dve.wait_ge(mid_ready, 2 * (n - 2) + s + 1)
                    nc.vector.scalar_tensor_tensor(res[:, n % 2, s], ps[:, 4 + 2 * s + n % 2, :], scale, pt[:, n, 0],
                                                   ALU.mult, ALU.subtract).then_inc(res_ready, 1)
                if n == NCH - 1:
                    dve.wait_ge(norm_psum, NCH)
                    nc.vector.tensor_reduce(norms[:, :], ps[:, 2:4, :], AX.X, ALU.max).then_inc(bound_ready, 1)
                for s, pt in enumerate((qparts, kparts)):
                    dve.wait_ge(mid_ready, 2 * n + s + 1)
                    nc.vector.tensor_tensor(pt[:, n, 2], res[:, n % 2, s], pt[:, n, 1], ALU.subtract).then_inc(parts_ready, 1)

            trail(ln1_stats, ln1_apply)
            each(split)
            dve.wait_ge(w_loaded, 16)
            nc.vector.tensor_scalar(omu[:, :], w[:, MU_R:MU_K + 1], -1.0, 1.0, ALU.mult, ALU.add)

            def stage_values(c, g, part):
                for a, b in runs(c, part):
                    ins = nc.vector.tensor_copy(vgrp[:, a:b, :], vaug[:, a:b, bass.ds(g * (4 * V1), 4 * V1)])
                ins.then_inc(v_staged, 1)

            nc.vector.memset(ot[:], 1.0).then_inc(ot_ready, 1)
            nc.vector.memset(o_inv[:], 1.0).then_inc(o_norm, 1)
            dve.wait_ge(ot_ready, 1)
            dve.wait_ge(o_norm, 1)
            dve.wait_ge(v_ready, NCH)
            stage_values(0, 0, 0)
            stage_values(0, 0, 1)

            dve.wait_ge(all_max, 1)
            nc.vector.tensor_scalar(flag[0:1, 0:1], norms_all[0:1, 0:1], norms_all[0:1, 1:2], BOUND ** 2,
                                    ALU.mult, ALU.is_le).then_inc(flag_ready, 1)
            dve.wait_ge(flag_ready, 1)
            small = dve.value_load(flag[0:1, 0:1], min_val=0, max_val=1)
            with dve.If(small == 0):
                nc.vector.memset(warm[:, 1:2], 0.0).then_inc(g_max, 2)
                for qb in range(TILES):
                    with dve.Fori(0, H // 2) as hp:
                        for i in range(2):
                            dve.wait_ge(g_scores, hp * 2 + (H * qb + i + 1))
                            row = qb // TPC * (H * TPC) + i * TPC + qb % TPC
                            nc.vector.tensor_reduce(negmax[:, bass.ds(hp * (2 * TPC) + row, 1)],
                                                    ps[:, 4 * i:4 * i + 4, :].rearrange("p b n -> p (b n)")[:, 0:(qb + 1) * P],
                                                    AX.X, ALU.max, negate=True).then_inc(g_max, 1)
                for a in range(2):
                    dve.wait_ge(g_turned, a + 1)
                    n1, n2, n3 = (nmp[:, a, j, :] for j in range(PARTS))
                    full, rest = nmt[:, a, 0, :], nmt[:, a, 1, :]
                    nc.vector.tensor_copy(full, ps[:, a, 0:P]).then_inc(g_step, 1)
                    dve.wait_ge(g_step, 4 * a + 1)
                    nc.vector.tensor_copy(n1, full).then_inc(g_step, 1)
                    dve.wait_ge(g_step, 4 * a + 2)
                    nc.vector.tensor_tensor(rest, full, n1, ALU.subtract).then_inc(g_step, 1)
                    dve.wait_ge(g_step, 4 * a + 3)
                    nc.vector.tensor_copy(n2, rest).then_inc(g_step, 1)
                    dve.wait_ge(g_step, 4 * a + 4)
                    nc.vector.tensor_tensor(n3, rest, n2, ALU.subtract).then_inc(g_parts, 1)

            def normalize(c, g):
                dve.wait_ge(o_turned, g + (G * c + 1))
                sums = ps[:, 7, :].rearrange("p (a r) -> p a r", r=32)
                nc.vector.reciprocal(o_inv[:], sums[:, :, HD]).then_inc(o_recip, 1)
                dve.wait_ge(o_recip, g + (G * c + 1))
                nc.vector.tensor_tensor(att[:, bass.ds(g * P + G * c * P, P)].rearrange("p (a v) -> p a v", v=HD), sums[:, :, 0:HD],
                                        o_inv[:].unsqueeze(2).broadcast_to([P, 4 * TPC, HD]), ALU.mult).then_inc(o_norm, 1)

            def group(c, g, nxt):
                k0 = g * kbs(c) + kbs_before(c)
                for i, (kb, w0) in enumerate(key_blocks(c)):
                    if kb < TPC * c:
                        continue
                    slot = probs_slot(i)[:, :, w0:w0 + P]
                    dve.wait_ge(exp_done, k0 * 2 + (3 + 2 * (i + 1)))
                    nc.vector.tensor_tensor(slot, slot, cs[:, C_TRI:C_TRI + P].unsqueeze(1).broadcast_to([P, 4, P]),
                                            ALU.min).then_inc(mask_done, 1)
                    if kb == TPC * c + 2:
                        normalize(c, g)
                if nxt is not None and nxt[0] == c:
                    dve.wait_ge(pv_done, k0 + (4 + first_part(c)))
                    stage_values(*nxt, 0)
                dve.wait_ge(pv_done, k0 + (4 + kbs(c)))
                nc.vector.tensor_copy(ot[:], ps[:, 6, :]).then_inc(ot_ready, 1)
                if nxt is not None:
                    if nxt[0] != c:
                        stage_values(*nxt, 0)
                    stage_values(*nxt, 1)

            for c in range(NCH):
                with dve.Fori(0, G - 1) as g:
                    group(c, g, (c, g + 1))
                group(c, G - 1, (c + 1, 0) if c + 1 < NCH else None)

            nc.vector.memset(vb[:, :, D:D + 1], 1.0)
            nc.vector.memset(xt_f[:, 0:1], 0.0)
            nc.vector.tensor_scalar(w_mu[:, 0], w[:, W_KK:W_KK + D], w[:, MU_K:MU_K + 1], None, ALU.mult)
            nc.vector.tensor_scalar(w_mu[:, 1], w[:, W_KK:W_KK + D], omu[:, 1:2], None, ALU.mult).then_inc(mu_ready, 1)
            normalize(NCH, 0)

            def add_y(n):
                dve.wait_ge(x_again[n], 16)
                dve.wait_ge(y_psum, n + 1)
                nc.vector.tensor_tensor(x[:, tiles(n), :], ps[:, high(n), :].rearrange("p (t d) -> p t d", t=TPC), x[:, tiles(n), :],
                                        ALU.add).then_inc(y_added, 1)
                dve.wait_ge(y_added, n + 1)
                ln_stats(LN2, n)

            def mix_r(f, n):
                dve.wait_ge(shifted, NCH * f + n + 1)
                nc.vector.scalar_tensor_tensor(mix_rt[:, cols(n)], xt_f[:, 1 + CH * n:1 + CH * (n + 1)], w[:, MU_R:MU_R + 1],
                                               prev_r[:, cols(n)], ALU.mult, ALU.add).then_inc(mixed, 1)

            def k_squared(f, n):
                dve.wait_ge(relu_ready, NCH * f + n + 1)
                nc.vector.scalar_tensor_tensor(kact[:, cols(n)], ps[:, high(n), :], 0.0, relu_k[:, cols(n)],
                                               ALU.max, ALU.mult).then_inc(kact_ready, 1)

            def add_mix(f, n, l):
                dve.wait_ge(gate_ready, NCH * f + n + 1)
                dve.wait_ge(fv_psum, NCH * f + n + 1)
                then(nc.vector.tensor_tensor(gate_r[:, cols(n)], ps[:, high(n), :], gate_r[:, cols(n)], ALU.mult))
                nc.vector.tensor_tensor(x[:, tiles(n), :], x[:, tiles(n), :], gate_r[:, cols(n)].rearrange("p (t d) -> p t d", t=TPC),
                                        ALU.add).then_inc(f_added, 1)
                if l is not None:
                    dve.wait_ge(f_added, NCH * f + n + 1)
                    ln_stats(l, n)

            def rope(s, n):
                rot, tmp_all, bank, c_cos, c_sin = ((q_rot, q_tmp, high(n), C_CQ, C_SQ), (k_rot, k_tmp, low(n), C_CK, C_SK))[s]
                dve.wait_ge((bq_psum, bk_psum)[s], n + 1)
                a = ps[:, bank, :].rearrange("p (t h e) -> p t h e", t=TPC, h=H)
                cos, sin = (cs[:, c0 + HD * TPC * n:c0 + HD * TPC * (n + 1)].rearrange("p (t e) -> p t e", t=TPC).unsqueeze(2)
                            for c0 in (c_cos, c_sin))
                r, tmp = (z[:, cols(n)].rearrange("p (t h e) -> p t h e", t=TPC, h=H) for z in (rot, tmp_all))
                e = HD // 2
                nc.vector.tensor_tensor(r, a, cos.broadcast_to([P, TPC, H, HD]), ALU.mult)
                nc.vector.tensor_tensor(tmp[:, :, :, 0:e], a[:, :, :, e:], sin[:, :, :, 0:e].broadcast_to([P, TPC, H, e]), ALU.mult)
                nc.vector.tensor_tensor(tmp[:, :, :, e:], a[:, :, :, 0:e], sin[:, :, :, e:].broadcast_to([P, TPC, H, e]),
                                        ALU.mult).then_inc((rot_parts_q, rot_parts_k)[s], 1)

            def features(n):
                for s, (e, r, feat) in enumerate(((q_exp, q_relu, q_feat), (k_exp, k_relu, k_feat))):
                    dve.wait_ge(feat_act, 4 * n + 2 * s + 2)
                    nc.vector.scalar_tensor_tensor(feat[:, cols(n)], e[:, cols(n)], 1.0, r[:, cols(n)],
                                                   ALU.min, ALU.add).then_inc(feat_ready, 1)

            each(add_y,
                 lambda n: mix_r(0, n),
                 lambda n: k_squared(0, n),
                 lambda n: add_mix(0, n, LN3))
            for n in range(NCH + 2):
                if n < NCH:
                    rope(0, n)
                    rope(1, n)
                if n >= 2:
                    features(n - 2)

            dve.wait_ge(kv_psum, 1)
            nc.vector.tensor_tensor(kvb[:, 0:D], ps[:, high(0), 0:D], cs[:, C_BLK:C_BLK + D], ALU.mult)
            nc.vector.tensor_scalar(kvb[:, D:D + H], cs[:, C_HM:C_HM + H], ps[:, high(0), D:D + 1], None, ALU.mult).then_inc(kv_ready, 1)

            def divide(n):
                dve.wait_ge(n_psum, n + 1)
                sums = ps[:, 2 * n:2 * n + 2, :].rearrange("p b (u m) -> p (b u) m", u=2)
                inv = rden[:, TPC * H * n:TPC * H * (n + 1)].rearrange("p (t h) -> p t h", h=H)
                then(nc.vector.tensor_scalar(inv, sums[:, :, D:D + H], 1e-6, None, ALU.max))
                then(nc.vector.reciprocal(inv, inv))
                nc.vector.tensor_tensor(heads_out[:, cols(n)].rearrange("p (t h v) -> p t h v", t=TPC, v=HD),
                                        sums[:, :, 0:D].rearrange("p t (h v) -> p t h v", v=HD),
                                        inv.unsqueeze(3).broadcast_to([P, TPC, H, HD]), ALU.mult).then_inc(n_ready, 1)

            def add_y2(n):
                dve.wait_ge(y2_psum, n + 1)
                nc.vector.tensor_tensor(x[:, tiles(n), :], ps[:, high(n), :].rearrange("p (t d) -> p t d", t=TPC), x[:, tiles(n), :],
                                        ALU.add).then_inc(y2_added, 1)
                dve.wait_ge(y2_added, n + 1)
                ln_stats(LN4, n)

            each(divide,
                 add_y2,
                 lambda n: mix_r(1, n),
                 lambda n: k_squared(1, n),
                 lambda n: add_mix(1, n, None))

        @block.tensor
        def _(pe):
            def turn(src, bank, done):
                for j in range(TPC):
                    ins = nc.tensor.transpose(ps[:, bank, P * j:P * (j + 1)], src[:, P * j:P * (j + 1)], ident)
                ins.then_inc(done, 1)

            def natural(bank, src, c0):
                for j in range(TPC):
                    ins = nc.tensor.matmul(ps[:, bank, P * j:P * (j + 1)], src[:, P * j:P * (j + 1)], w[:, c0:c0 + D],
                                           start=True, stop=True)
                return ins

            def turn_ln1(n):
                pe.wait_ge(ln1_ready[n], 1)
                at_least(pe, xt_ready[LN1], n)
                turn(xh_a[:, cols(n)], 0, xt_psum[LN1])

            def qkv(n):
                pe.wait_ge(xt_ready[LN1], n + 1)
                if n >= 2:
                    pe.wait_ge(res_ready, 2 * (n - 1))
                src = xt_a[:, cols(n)]
                nc.tensor.matmul(ps[:, 4 + n % 2, :], w[:, W_Q:W_Q + D], src, start=True, stop=True).then_inc(qkv_psum, 1)
                nc.tensor.matmul(ps[:, 6 + n % 2, :], w[:, W_K:W_K + D], src, start=True, stop=True).then_inc(qkv_psum, 1)
                at_least(pe, v_ready, n)
                natural(1, src, W_V).then_inc(qkv_psum, 1)

            pe.wait_ge(c_loaded, 16)
            nc.tensor.transpose(ps[:, 7, 0:P], ident, ident).then_inc(pv_done, 4)
            for _ in range(WARM_UP):
                nc.tensor.matmul(ps[:, 7, :], ident, cs[:, 0:CH], start=True, stop=True)
            pe.wait_ge(w_loaded, 16)

            def square_norms(n):
                pe.wait_ge(hi_ready, 2 * n + 2)
                for s in range(2):
                    ins = nc.tensor.matmul(ps[32 * n:32 * (n + 1), 2 + s, :], cb[:, B_HN:B_HN + 32], sq[:, n % 2, s],
                                           start=True, stop=True)
                ins.then_inc(norm_psum, 1)

            turn_ln1(0)
            for n in range(NCH):
                if n + 1 < NCH:
                    turn_ln1(n + 1)
                qkv(n)
                if n == 0:
                    pe.wait_ge(cb_loaded, 16)
                else:
                    square_norms(n - 1)
            square_norms(NCH - 1)

            pe.wait_ge(flag_ready, 1)
            small = pe.value_load(flag[0:1, 0:1], min_val=0, max_val=1)
            with pe.If(small == 0):
                pe.wait_ge(v_ready, NCH)
                for n in range(NCH):
                    pe.wait_ge(qk_loaded[n], QK_LOADS)
                for qb in range(TILES):
                    with pe.Fori(0, H // 2) as hp:
                        for i in range(2):
                            head = hp * (2 * CH) + i * CH
                            pe.wait_ge(g_max, hp * 2 + (H * qb + i + 1))
                            for k0 in range(0, (qb + 1) * P, CH):
                                k1 = min(k0 + CH, (qb + 1) * P)
                                bank = 4 * i + k0 // CH
                                ins = nc.tensor.matmul(ps[:, bank, 0:k1 - k0],
                                                       qq[0:SHIFT_ROW, bass.ds(head + (H * CH * (qb // TPC) + P * (qb % TPC)), P)],
                                                       kk[0:SHIFT_ROW, bass.ds(head + H * k0, k1 - k0)],
                                                       start=True, stop=True)
                            ins = nc.tensor.matmul(ps[:, bank, k1 - k0 - P:k1 - k0], cb[:, B_ID:B_ID + P], cb[:, B_TRI:B_TRI + P],
                                                   start=False, stop=True, skip_group_check=True)
                            ins.then_inc(g_scores, 1)
                pe.wait_ge(g_max, H * TILES + 2)
                for a in range(2):
                    nc.tensor.transpose(ps[:, a, 0:P], negmax[:, P * a:P * (a + 1)], ident).then_inc(g_turned, 1)
                pe.wait_ge(g_parts, 2)
                pe.wait_ge(g_rows, 16)

            def score(c, g, i):
                kb, w0 = key_blocks(c)[i]
                k0 = g * kbs(c) + kbs_before(c)
                for u in range(2):
                    n = 2 * i + u
                    pe.wait_ge(exp_done, k0 * 2 + (n - back(c, n) + 4))
                    for v in range(2):
                        head = g * (4 * CH) + (2 * u + v) * CH
                        ins = nc.tensor.matmul(ps[:, 2 * score_buffer(c, n) + v, w0:CH], kk[0:ROWS, bass.ds(head + (H * CH * (kb // TPC) + P * (kb % TPC)), P)],
                                               qq[0:ROWS, bass.ds(head + (H * CH * c + w0), CH - w0)], start=True, stop=True)
                    ins.then_inc(s_done, 1)

            def weigh(c, g, i):
                kb, w0 = key_blocks(c)[i]
                k0 = g * kbs(c) + kbs_before(c)
                if i == 0:
                    pe.wait_ge(v_staged, g * 2 + (2 * G * c + 1))
                    pe.wait_ge(ot_ready, g + (G * c + 1))
                if i == first_part(c):
                    pe.wait_ge(v_staged, g * 2 + (2 * G * c + 2))
                pe.wait_ge(exp_done, k0 * 2 + (3 + 2 * (i + 1)))
                if kb >= TPC * c:
                    pe.wait_ge(mask_done, g * TPC + (TPC * G * c + kb - TPC * c + 1))
                for v in range(4):
                    ins = nc.tensor.matmul(ps[32 * v:32 * v + V1, 6, w0:CH], vgrp[:, kb, V1 * v:V1 * (v + 1)], probs_slot(i)[:, v, w0:CH],
                                           start=(i == 0), stop=(c == 0 or i == kbs(c) - 1), skip_group_check=True)
                ins.then_inc(pv_done, 1)

            def turn_sums(c, g):
                pe.wait_ge(ot_ready, g + (G * c + 1))
                pe.wait_ge(o_norm, g + (G * c + 1))
                for j in range(TPC):
                    ins = nc.tensor.transpose(ps[:, 7, P * j:P * (j + 1)], ot[:, P * j:P * (j + 1)], ident)
                ins.then_inc(o_turned, 1)

            def group(c, g, nxt):
                for i in range(2, kbs(c)):
                    score(c, g, i)
                    weigh(c, g, i - 2)
                    if i == 2:
                        turn_sums(c, g)
                if nxt is not None and nxt[0] != c:
                    pe.wait_ge(qk_loaded[nxt[0]], QK_LOADS)
                for j in range(2):
                    if nxt is not None:
                        score(*nxt, j)
                    weigh(c, g, kbs(c) - 2 + j)

            pe.wait_ge(v_ready, NCH)
            pe.wait_ge(res_ready, 2 * NCH)
            pe.wait_ge(bound_ready, 1)
            pe.wait_ge(qk_loaded[0], QK_LOADS)
            score(0, 0, 0)
            score(0, 0, 1)
            for c in range(NCH):
                with pe.Fori(0, G - 1) as g:
                    group(c, g, (c, g + 1))
                group(c, G - 1, (c + 1, 0) if c + 1 < NCH else None)

            def stage(ready, free):
                for s, count in (ready, free):
                    at_least(pe, s, count)

            def turn_att(n):
                stage((o_norm, G * (n + 1) + 2), (exp_done, 3 + 2 * kbs_before(NCH)))
                for j in range(TPC):
                    for g in range(G):
                        a = P * (1 + G * n + g) + 32 * j
                        ins = nc.tensor.matmul(ps[32 * g:32 * (g + 1), low(n), P * j:P * (j + 1)], att[:, a:a + 32], ident,
                                               start=True, stop=True)
                ins.then_inc(att_psum, 1)

            def project(n):
                stage((att_ready, n + 1), (o_norm, G * NCH + 2) if n == NCH - 1 else (ot_ready, G * NCH + 1))
                natural(high(n), att_t[:, cols(n)], W_O).then_inc(y_psum, 1)

            def turn_ln2(n):
                stage((xh_ready[LN2], n + 1), (att_ready, n + 1))
                turn(xh[:, cols(n)], low(n), xt_psum[LN2])

            def mix_k_in(f, n):
                stage((xt_ready[(LN2, LN4)[f]], n + 1), ((y_added, y2_added)[f], n + 1))
                pe.wait_ge(mu_ready, 1)
                for i in range(2):
                    ins = nc.tensor.matmul(ps[:, high(n), :], w_mu[:, i], xt_f[:, CH * n + 1 - i:CH * (n + 1) + 1 - i],
                                           start=(i == 0), stop=(i == 1))
                ins.then_inc(fk_psum, 1)

            def mix_r_in(f, n):
                stage((mixed, NCH * f + n + 1), (xt_ready[(LN2, LN4)[f]], n + 1))
                ins = natural(low(n), mix_rt[:, cols(n)], W_R)
                ins.then_inc(fr_psum, 1)

            def mix_out(f, n):
                stage((kact_ready, NCH * f + n + 1), (kact_ready, NCH * f + n + 1))
                natural(high(n), kact[:, cols(n)], W_VV).then_inc(fv_psum, 1)

            def turn_ln3(n):
                stage((xh_ready[LN3], n + 1), (gate_ready, n + 1))
                turn(xh[:, cols(n)], low(n), xt_psum[LN3])

            def q_b(n):
                stage((xt_ready[LN3], n + 1), (f_added, n + 1))
                natural(high(n), xt_b[:, cols(n)], W_QKV).then_inc(bq_psum, 1)

            def k_b(n):
                stage((xt_ready[LN3], n + 1), (xt_ready[LN3], n + 1))
                natural(low(n), xt_b[:, cols(n)], W_QKV + D).then_inc(bk_psum, 1)

            def v_b(n):
                stage((xt_ready[LN3], n + 1), (rot_parts_q, n + 1))
                natural(high(n), xt_b[:, cols(n)], W_QKV + 2 * D).then_inc(bv_psum, 1)

            def turn_q(n):
                stage((feat_ready, 2 * n + 1), (rot_parts_k, n + 1))
                turn(q_feat[:, cols(n)], low(n), qft_psum)

            def summarize(n):
                stage((feat_ready, 2 * n + 2), (bv_ready, NCH))
                for j in range(TPC):
                    t = TPC * n + j
                    ins = nc.tensor.matmul(ps[:, high(0), 0:D + 1], k_feat[:, P * t:P * (t + 1)], vb[:, t, :],
                                           start=(t == 0), stop=(t == TILES - 1))
                if n == NCH - 1:
                    ins.then_inc(kv_psum, 1)

            def numerators(n):
                stage((kv_ready, 1), (qft_ready, NCH))
                for j in range(TPC):
                    t = TPC * n + j
                    ins = nc.tensor.matmul(ps[:, t // 2, t % 2 * (CH // 2):t % 2 * (CH // 2) + D + H], qft[:, P * t:P * (t + 1)],
                                           kvb[:, 0:D + H], start=True, stop=True)
                ins.then_inc(n_psum, 1)

            def turn_heads(n):
                stage((n_ready, n + 1), (n_ready, NCH))
                turn(heads_out[:, cols(n)], low(n), nt_psum)

            def project_b(n):
                stage((nt_ready, n + 1), (n_ready, NCH))
                natural(high(n), att_t[:, cols(n)], W_OUT).then_inc(y2_psum, 1)

            def turn_ln4(n):
                stage((xh_ready[LN4], n + 1), (nt_ready, n + 1))
                turn(xh[:, cols(n)], low(n), xt_psum[LN4])

            turn_att(0)
            turn_att(1)
            project(0)
            turn_sums(NCH, 0)
            project(1)
            for n in range(2, NCH):
                turn_att(n)
                project(n)
            trail(turn_ln2, lambda n: mix_k_in(0, n))
            each(lambda n: mix_r_in(0, n), lambda n: mix_out(0, n))
            trail(turn_ln3, lambda n: (q_b(n), k_b(n)))
            each(v_b, turn_q, summarize,
                 numerators, turn_heads, project_b)
            trail(turn_ln4, lambda n: mix_k_in(1, n))
            each(lambda n: mix_r_in(1, n), lambda n: mix_out(1, n))


def constants():
    f = np.float32

    def high(a):
        return (np.ascontiguousarray(a, f).view(np.uint32) & np.uint32(0xFFFF0000)).view(f)

    def bits(a):
        return (np.ascontiguousarray(a, f).view(np.uint32) >> np.uint32(16)).astype(np.uint16)

    c = np.zeros((P, N_C), f)
    c[:, C_ID:C_ID + P] = np.eye(P)
    k, q = np.arange(P)[:, None], np.arange(P)[None, :]
    c[:, C_TRI:C_TRI + P] = np.where(k <= q, f(3e38), f(0))
    c[:, C_BLK:C_BLK + P] = k // HD == q // HD
    c[:, C_HM:C_HM + H] = k // HD == np.arange(H)[None, :]
    inv = (1.0 / f(10000.0) ** (np.arange(0, HD, 2, dtype=f) / f(HD))).astype(f)
    ang = np.arange(T, dtype=f)[:, None] * inv[None, :]
    cos, sin = np.cos(ang), np.sin(ang)
    cos, sin = np.concatenate([cos, cos], 1), np.concatenate([-sin, sin], 1)
    for base, tab, s in ((C_CQ, cos, HD ** -0.5), (C_SQ, sin, HD ** -0.5), (C_CK, cos, 1.0), (C_SK, sin, 1.0)):
        c[:, base:base + TILES * HD] = (tab * f(s)).reshape(TILES, P, HD).transpose(1, 0, 2).reshape(P, -1)
    cb = np.zeros((P, N_B), f)
    cb[:, B_ID:B_ID + P] = np.eye(P)
    cb[:, B_TRI:B_TRI + P] = np.where(q > k, -1e30, 0.0)
    cb[:, B_HN:B_HN + H] = k % H == np.arange(H)[None, :]
    slopes = (f(1.0) / f(256.0) ** ((np.arange(H, dtype=f) + f(1)) / f(H))).astype(f)
    parts, rest = [], slopes
    for _ in range(PARTS):
        part = high(rest)
        parts.append(part)
        rest = rest - part
    pos = np.arange(T)
    hi, lo = pos // P * P, pos % P
    krows, qrows = np.zeros((CONST_ROWS, H, T), f), np.zeros((CONST_ROWS, H, T), f)
    for j, part in enumerate(parts):
        r = 4 * j
        krows[r], qrows[r] = hi[None, :], part[:, None]
        krows[r + 1], qrows[r + 1] = part[:, None], -hi[None, :]
        krows[r + 2], qrows[r + 2] = lo[None, :], part[:, None]
        krows[r + 3], qrows[r + 3] = part[:, None], -lo[None, :]
    krows[SHIFT_ROW - PAIR_ROWS:] = 1.0
    qrows[SHIFT_ROW - PAIR_ROWS] = -SHIFT
    krows, qrows = (r.reshape(CONST_ROWS, H, NCH, CH).transpose(0, 2, 1, 3).reshape(CONST_ROWS, H * T) for r in (krows, qrows))
    return c, bits(cb), bits(krows), bits(qrows)


def kernel(L0_attn_a_x, L0_attn_a_W_Q, L0_attn_a_W_K, L0_attn_a_W_V, L0_attn_a_W_O, L0_attn_b_w_qkv, L0_attn_b_w_out,
           L0_ffn_W_r, L0_ffn_W_k, L0_ffn_W_v, L0_ffn_mu_r, L0_ffn_mu_k):
    import concourse.bacc as bacc
    from concourse.bass_utils import run_bass_kernel_spmd

    nc = bacc.Bacc("TRN2", target_bir_lowering=False, num_devices=1)
    w_q, w_k = (np.asarray(m).reshape(H, HD, D).transpose(1, 0, 2).reshape(D, D) for m in (L0_attn_a_W_Q, L0_attn_a_W_K))
    weights = np.concatenate(
        [np.asarray(m).T for m in (w_q, w_k, L0_attn_a_W_V, L0_attn_a_W_O, L0_ffn_W_r, L0_ffn_W_k,
                                   L0_ffn_W_v, L0_attn_b_w_qkv, L0_attn_b_w_out)]
        + [np.asarray(L0_ffn_mu_r)[:, None], np.asarray(L0_ffn_mu_k)[:, None]], axis=1)
    consts, consts_b, krows, qrows = constants()
    arrays = {
        "in_x": np.ascontiguousarray(np.asarray(L0_attn_a_x).reshape(T, D)),
        "in_weights": np.ascontiguousarray(weights),
        "in_consts": consts, "in_consts_b": consts_b, "in_krows": krows, "in_qrows": qrows,
    }
    args = [nc.dram_tensor(name, a.shape, mybir.dt.from_np(a.dtype), kind="ExternalInput").ap() for name, a in arrays.items()]
    out = nc.dram_tensor("out_y", (T, D), F32, kind="ExternalOutput").ap()
    program(nc, *args, out)
    r = run_bass_kernel_spmd(nc, [arrays], core_ids=[0])
    return r.results[0]["out_y"].reshape(1, T, D)
```

```python
from contextlib import ExitStack

import numpy as np

import concourse.bass as bass
from concourse import mybir

F32 = mybir.dt.float32
BF16 = mybir.dt.bfloat16
I32 = mybir.dt.int32
ALU = mybir.AluOpType
ACT = mybir.ActivationFunctionType
AX = mybir.AxisListType
RMAX = bass.bass_isa.ReduceOp.max

P = 128
T = 2048
D = 128
H = 16
HD = D // H
TILES = T // P
CH = 512
NCH = T // CH
TPC = CH // P
G = H // 4
EPS = 1e-5
PARTS = 3
PAIR_ROWS = PARTS * PARTS * HD
POS_ROWS = 12
SHIFT_ROW = 96
ROWS = SHIFT_ROW + PARTS
CONST_ROWS = ROWS - PAIR_ROWS
SHIFT = 32.0
BOUND = 30.0
V1 = HD + 1
WARM_UP = 2

W_Q, W_K, W_V, W_O, W_R, W_KK, W_VV, W_QKV, W_OUT, MU_R, MU_K = (
    0, 128, 256, 384, 512, 640, 768, 896, 1280, 1408, 1409)
N_W = 1410
C_ID, C_TRI, C_BLK, C_HM, C_CQ, C_SQ, C_CK, C_SK = 0, 128, 256, 384, 400, 528, 656, 784
N_C = 912
B_ID, B_TRI, B_HN = 0, 128, 256
N_B = 288


def program(nc, x_in, w_in, c_in, cb_in, krow_in, qrow_in, out):
    with ExitStack() as ctx:
        def sb(name, shape, dt):
            return ctx.enter_context(nc.sbuf_tensor(name, shape, dt))

        def sem(name):
            return ctx.enter_context(nc.semaphore(name))

        ps = ctx.enter_context(nc.psum_tensor("ps", [P, 8, CH], F32))

        kk = sb("kk", [P, H * T], BF16)
        qq = sb("qq", [P, H * T], BF16)
        probs = sb("probs", [P, 3 * 4 * CH], F32)
        x = sb("x", [P, TILES, D], F32)
        vaug = sb("vaug", [P, TILES, H * V1], F32)
        vgrp_area = sb("vgrp_area", [P, 2 * CH], F32)
        vgrp = vgrp_area[:, 0:TILES * 4 * V1].rearrange("p (t v) -> p t v", t=TILES)
        ot = sb("ot", [P, CH], F32)
        o_inv = sb("o_inv", [P, 4 * TPC], F32)
        att = sb("att", [P, (1 + NCH * G) * TPC * 4 * HD], F32)
        w = sb("w", [P, N_W], F32)
        cs = sb("cs", [P, N_C], F32)
        cb = sb("cb", [P, N_B], BF16)
        stats = sb("stats", [P, NCH, TPC, 6], F32)
        mv = sb("mv", [P, NCH, TPC, 2], F32)
        veps = sb("veps", [P, NCH, TPC], F32)
        rstd = sb("rstd", [P, NCH, TPC], F32)
        negmean = sb("negmean", [P, NCH, TPC], F32)
        shift_by = sb("shift_by", [P, NCH, TPC], F32)
        neghalf = sb("neghalf", [P, TPC], F32)
        norms = sb("norms", [P, 2], F32)
        norms_all = sb("norms_all", [P, 2], F32)
        flag = sb("flag", [1, 1], I32)
        warm = sb("warm", [P, 2], F32)
        negmax = sb("negmax", [P, H * TILES], F32)
        nmp = sb("nmp", [P, 2, PARTS, P], BF16)
        omu = sb("omu", [P, 2], F32)
        rden = sb("rden", [P, TILES * H], F32)

        xt_a = probs[:, 0:T]
        xh_a = probs[:, T:2 * T]
        res = probs[:, 2 * T:3 * T].rearrange("p (b s n) -> p b s n", b=2, s=2)
        sq = vgrp_area[:, 0:2 * CH].bitcast(BF16).rearrange("p (b s n) -> p b s n", b=2, s=2)
        qparts, kparts = (a[:, H * CH * (NCH - 1):][:, 0:NCH * PARTS * CH].rearrange("p (n j t) -> p n j t", n=NCH, j=PARTS)
                          for a in (qq, kk))
        kk32 = kk[:, :].bitcast(F32)
        qq32 = qq[:, :].bitcast(F32)
        area = [kk32[:, T * i:T * (i + 1)] for i in range(8)] + [qq32[:, T * i:T * (i + 1)] for i in range(5)]
        (att_t, xh, prev_r, prev_k, mix_rt, mix_k, relu_k, kact, gate_r, spare, xt_b, q_tmp, qft) = area
        k_rot, k_exp, k_relu, k_feat = gate_r, spare, relu_k, kact
        q_rot, q_exp, q_relu, q_feat = prev_r, prev_k, mix_rt, mix_k
        heads_out = mix_k
        k_tmp = att_t
        xt_f = qq32[:, 5 * T:6 * T + 1]
        vb = qq32[:, 6 * T + 8:6 * T + 8 + TILES * (D + 1)].rearrange("p (t n) -> p t n", t=TILES)
        kvb = qq32[:, 7 * T + CH:7 * T + CH + D + H]
        w_mu = qq32[:, 7 * T + 2 * CH:7 * T + 2 * CH + 2 * D].rearrange("p (i n) -> p i n", i=2)
        nmt = probs[:, 0:4 * P].rearrange("p (a b q) -> p a b q", a=2, b=2)

        qs = nc.dram_tensor("qs", [NCH, PARTS, HD, H, CH], BF16, kind="Internal").ap()
        ks = nc.dram_tensor("ks", [NCH, PARTS, HD, H, CH], BF16, kind="Internal").ap()
        ms = nc.dram_tensor("ms", [2, P, PARTS, P], BF16, kind="Internal").ap()

        def sems(names):
            return [sem(s) for s in names.split()]

        x_loaded = [sem(f"x_loaded{n}") for n in range(NCH)]
        x_again = [sem(f"x_again{n}") for n in range(NCH)]
        qk_loaded = [sem(f"qk_loaded{n}") for n in range(NCH)]
        const_loaded = [sem(f"const_loaded{n}") for n in range(NCH)]
        first_loaded = sem("first_loaded")
        w_loaded, c_loaded, cb_loaded, stored = sems("w_loaded c_loaded cb_loaded stored")
        parts_out = [sem(f"parts_out{n}") for n in range(NCH)]
        ln1_ready = [sem(f"ln1_ready{n}") for n in range(NCH)]
        pool_ready, dve_step = sems("pool_ready dve_step")
        ln_var, ln_rstd, ln_shift, xh_ready, xt_psum, xt_ready = (
            [sem(f"{s}{i}") for i in range(4)] for s in ("ln_var", "ln_rstd", "ln_shift", "xh_ready", "xt_psum", "xt_ready"))
        qk_psum, v_psum, hi_ready, res_ready, mid_ready, parts_ready, v_ready = sems(
            "qk_psum v_psum hi_ready res_ready mid_ready parts_ready v_ready")
        norm_psum, squares, bound_ready, all_max, flag_ready, g_scores, g_max, g_turned, g_parts, g_stored, g_rows, g_step = sems(
            "norm_psum squares bound_ready all_max flag_ready g_scores g_max g_turned g_parts g_stored g_rows g_step")
        s_done, exp_done, mask_done, pv_done, v_staged, ot_ready, o_turned, o_recip, o_norm = sems(
            "s_done exp_done mask_done pv_done v_staged ot_ready o_turned o_recip o_norm")
        att_psum, att_ready, y_psum, y_added = sems("att_psum att_ready y_psum y_added")
        mu_ready, shifted, mixed, fk_psum, fr_psum, relu_ready, gate_ready, kact_ready, fv_psum, f_added = sems(
            "mu_ready shifted mixed fk_psum fr_psum relu_ready gate_ready kact_ready fv_psum f_added")
        bq_psum, bk_psum, bv_psum, rot_parts_q, rot_parts_k, bv_ready, rot_ready, rot_last, feat_act, feat_ready, qft_psum, qft_ready, kv_psum, kv_ready = sems(
            "bq_psum bk_psum bv_psum rot_parts_q rot_parts_k bv_ready rot_ready rot_last feat_act feat_ready qft_psum qft_ready kv_psum kv_ready")
        n_psum, n_ready, nt_psum, nt_ready, y2_psum, y2_added = sems("n_psum n_ready nt_psum nt_ready y2_psum y2_added")

        ident = cs[:, C_ID:C_ID + P]
        block = ctx.enter_context(nc.Block())

        def kbs(c):
            return TPC * (c + 1)

        def kbs_before(c):
            return sum(G * kbs(i) for i in range(c))

        def score_buffer(c, n):
            return 1 if n == 2 * kbs(c) - 1 and n % 3 == 0 else n % 3

        def back(c, n):
            b = score_buffer(c, n)
            here = [n - m for m in range(n) if score_buffer(c, m) == b]
            before = [n + 2 * kbs(i) - m for i in (c, max(c - 1, 0)) for m in range(2 * kbs(i)) if score_buffer(i, m) == b]
            return min(here or before)

        def probs_slot(i):
            if i % 4 == 1:
                return x[:, :, :].rearrange("p t d -> p (t d)").rearrange("p (h q) -> p h q", h=4)
            k = (0, 0, 1, 2)[i % 4]
            return probs[:, k * 4 * CH:(k + 1) * 4 * CH].rearrange("p (h q) -> p h q", h=4)

        def at_least(eng, s, count):
            if count > 0:
                eng.wait_ge(s, count)

        def cols(n):
            return slice(CH * n, CH * (n + 1))

        def tiles(n):
            return slice(TPC * n, TPC * (n + 1))

        def ln_apply(engine, waits, l, n, dst):
            waits.wait_ge(ln_rstd[l], n + 1)
            for j in range(TPC):
                ins = engine.tensor_scalar(dst[:, P * j:P * (j + 1)], x[:, TPC * n + j, :], negmean[:, n, j:j + 1],
                                           rstd[:, n, j:j + 1], ALU.add, ALU.mult)
            ins.then_inc(xh_ready[l] if l != LN1 else ln1_ready[n], 1)

        def each(*stages):
            for stage in stages:
                for n in range(NCH):
                    stage(n)

        def in_turn(*stages):
            for n in range(NCH + len(stages) - 1):
                for i, stage in enumerate(stages):
                    if stage and 0 <= n - i < NCH:
                        stage(n - i)

        def but_first(stage):
            return lambda n: stage(n) if n else None

        def trail(first, second):
            for n in range(NCH + 1):
                if n < NCH:
                    first(n)
                if n:
                    second(n - 1)

        def low(n):
            return n

        def high(n):
            return 4 + n

        def key_blocks(c):
            full = [(kb, 0) for kb in range(TPC * c)]
            diagonal = [(TPC * c + j, P * j) for j in range(TPC)]
            if not full:
                return diagonal
            order = [b for pair in zip(full[:TPC - 1], diagonal) for b in pair]
            return order + diagonal[TPC - 1:] + full[TPC - 1:]

        def first_part(c):
            return kbs(c) // 2

        def runs(c, part):
            order, half = [kb for kb, _ in key_blocks(c)], first_part(c)
            found = []
            for kb in sorted((order[:half], order[half:])[part]):
                if found and found[-1][1] == kb:
                    found[-1][1] = kb + 1
                else:
                    found.append([kb, kb + 1])
            return found

        def masked(c, i):
            return sum(kb >= TPC * c for kb, _ in key_blocks(c)[:i + 1])

        LN1, LN2, LN3, LN4 = range(4)
        QK_LOADS = 16 * (PARTS + 1)
        CONST_LOADS = 16 * 2

        @block.sync
        def _(sp):
            xd = x_in.rearrange("(t p) d -> p t d", p=P)
            for n in range(NCH):
                sp.dma_start(x[:, tiles(n), :], xd[:, tiles(n), :]).then_inc(x_loaded[n], 16)
                if n == 0:
                    sp.dma_start(cs[:, :], c_in).then_inc(c_loaded, 16)
                if n == 1:
                    sp.dma_start(w[:, :], w_in).then_inc(w_loaded, 16)
            sp.dma_start(cb[:, :], cb_in.bitcast(BF16)).then_inc(cb_loaded, 16)
            block_cols = H * CH

            def constant_rows(n):
                a, b = block_cols * n, block_cols * (n + 1)
                sp.dma_start(kk[PAIR_ROWS:ROWS, a:b], krow_in.bitcast(BF16)[:, a:b]).then_inc(const_loaded[n], 16)
                sp.dma_start(qq[PAIR_ROWS:ROWS, a:b], qrow_in.bitcast(BF16)[:, a:b]).then_inc(const_loaded[n], 16)

            def parts_to_dram(n):
                sp.wait_ge(parts_ready, 2 * n + 1)
                sp.dma_start(qs[n].rearrange("j d h t -> (d h) j t"), qparts[:, n]).then_inc(parts_out[n], 16)
                sp.wait_ge(parts_ready, 2 * n + 2)
                sp.dma_start(ks[n].rearrange("j d h t -> (d h) j t"), kparts[:, n]).then_inc(parts_out[n], 16)

            def rows_from_dram(n, h0, h1, done):
                sp.wait_ge(parts_out[n], 32)
                a, size = block_cols * n + h0 * CH, (h1 - h0) * CH
                q_part = qs[n, :, :, h0:h1].rearrange("j d h t -> (j d) (h t)").unsqueeze(0).broadcast_to([PARTS, PARTS * HD, size])
                sp.dma_start(qq[0:PAIR_ROWS, a:a + size], q_part).then_inc(done, 16)
                for i in range(PARTS):
                    r = PARTS * HD * i
                    k_part = ks[n, i, :, h0:h1].rearrange("d h t -> d (h t)").unsqueeze(0).broadcast_to([PARTS, HD, size])
                    sp.dma_start(kk[r:r + PARTS * HD, a:a + size], k_part).then_inc(done, 16)

            for n in range(NCH - 1):
                constant_rows(n)
            parts_to_dram(0)
            rows_from_dram(0, 0, 4, first_loaded)
            rows_from_dram(0, 4, H, qk_loaded[0])
            for n in range(1, NCH):
                parts_to_dram(n)
            for n in range(1, NCH):
                rows_from_dram(n, 0, H, qk_loaded[n])
            constant_rows(NCH - 1)
            sp.wait_ge(flag_ready, 1)
            small = sp.value_load(flag[0:1, 0:1], min_val=0, max_val=1)
            with sp.If(small == 0):
                sp.wait_ge(g_parts, 2)
                sp.dma_start(ms.rearrange("a p j q -> p a (j q)"), nmp[:, :, :, :].rearrange("p a j q -> p a (j q)")).then_inc(g_stored, 16)
                sp.wait_ge(g_stored, 16)
                sp.dma_start(qq[SHIFT_ROW:ROWS, :].rearrange("j (r q) -> j r q", q=P), ms.rearrange("a p j q -> j (a p) q")).then_inc(g_rows, 16)
            sp.wait_ge(pv_done, 4 + kbs_before(NCH) - 2)
            for n in range(NCH):
                sp.dma_start(x[:, tiles(n), :], xd[:, tiles(n), :]).then_inc(x_again[n], 16)
            od = out.rearrange("(t p) d -> p t d", p=P)
            for n in range(NCH):
                sp.wait_ge(f_added, NCH + n + 1)
                sp.dma_start(od[:, tiles(n), :], x[:, tiles(n), :]).then_inc(stored, 16)
            sp.wait_ge(stored, 16 * NCH)

        @block.gpsimd
        def _(pool):
            nc.gpsimd.memset(neghalf[:], -0.5).then_inc(pool_ready, 1)
            nc.gpsimd.memset(vaug[:], 1.0).then_inc(pool_ready, 1)
            pool.wait_ge(pool_ready, 1)

            def rstd_of(l, n):
                pool.wait_ge(ln_var[l], n + 1)
                nc.gpsimd.tensor_tensor(rstd[:, n], veps[:, n], neghalf[:], ALU.pow).then_inc(ln_rstd[l], 1)

            def shift_of(l, n):
                rstd_of(l, n)
                pool.wait_ge(ln_rstd[l], n + 1)
                nc.gpsimd.tensor_tensor(shift_by[:, n], negmean[:, n], rstd[:, n], ALU.mult).then_inc(ln_shift[l], 1)

            def shift(f, n):
                pool.wait_ge(xt_ready[(LN2, LN4)[f]], n + 1)
                nc.gpsimd.tensor_scalar(prev_r[:, cols(n)], xt_f[:, cols(n)], omu[:, 0:1], 0.0, ALU.mult, ALU.add).then_inc(shifted, 1)

            def turned_qk(n):
                for s, (a, b) in enumerate(((q_rot, q_tmp), (k_rot, k_tmp))):
                    pool.wait_ge((rot_parts_q, rot_parts_k)[s], n + 1)
                    nc.gpsimd.tensor_tensor(a[:, cols(n)], a[:, cols(n)], b[:, cols(n)], ALU.add).then_inc(rot_ready, 1)

            def middle_parts(n):
                for s, pt in ((0, qparts), (1, kparts)):
                    pool.wait_ge(res_ready, 2 * n + s + 1)
                    nc.gpsimd.tensor_scalar(pt[:, n, 1], res[:, n % 2, s], 1.0, 0.0, ALU.mult, ALU.add).then_inc(mid_ready, 1)

            for n in range(NCH):
                rstd_of(LN1, n)
                if n % 2:
                    ln_apply(nc.gpsimd, pool, LN1, n, xh_a[:, cols(n)])
            each(middle_parts)
            pool.wait_ge(bound_ready, 1)
            nc.gpsimd.partition_all_reduce(norms_all[:], norms[:], P, RMAX).then_inc(all_max, 1)

            each(lambda n: shift_of(LN2, n), lambda n: shift(0, n))
            each(lambda n: shift_of(LN3, n))
            for n in range(NCH - 1):
                turned_qk(n)
            each(lambda n: shift_of(LN4, n), lambda n: shift(1, n))

        @block.scalar
        def _(act):
            act.wait_ge(pool_ready, 1)
            nc.scalar.activation(warm[:, 0:1], neghalf[:, 0:1], ACT.Exp).then_inc(exp_done, 3)

            def turned(psum, ready, n, bank, dst):
                act.wait_ge(psum, n + 1)
                nc.scalar.copy(dst, ps[:, bank, :]).then_inc(ready, 1)

            def take_part(n, s):
                at_least(act, norm_psum, n - 1)
                pt, scale, b = ((qparts, float(HD) ** -0.5), (kparts, 1.0))[s] + (4 + 2 * s + n % 2,)
                act.wait_ge(qk_psum, 2 * n + s + 1)
                nc.scalar.activation(pt[:, n, 0], ps[:, b, :], ACT.Copy, scale=scale)
                nc.scalar.activation(sq[:, n % 2, s], ps[:, b, :], ACT.Square, scale=scale).then_inc(hi_ready, 1)

            def take_values(n):
                act.wait_ge(v_psum, n + 1)
                act.wait_ge(pool_ready, 2)
                nc.scalar.copy(vaug[:, tiles(n), 0:H * V1].rearrange("p t (h v) -> p t h v", h=H)[:, :, :, 0:HD],
                               ps[:, n % 2, :].rearrange("p (t h v) -> p t h v", t=TPC, h=H)).then_inc(v_ready, 1)

            def take_xt(n):
                turned(xt_psum[LN1], xt_ready[LN1], n, 0, xt_a[:, cols(n)])

            take_xt(0)
            for n in range(NCH):
                take_part(n, 0)
                if n + 1 < NCH:
                    take_xt(n + 1)
                take_part(n, 1)
            each(take_values)

            def exps(c, g):
                k0 = g * kbs(c) + kbs_before(c)
                for i, (kb, w0) in enumerate(key_blocks(c)):
                    slot = probs_slot(i)
                    for u in range(2):
                        n = 2 * i + u
                        if u == 0:
                            act.wait_ge(pv_done, k0 + (i + 1))
                        act.wait_ge(s_done, k0 * 2 + n + 1)
                        b = 2 * score_buffer(c, n)
                        nc.scalar.activation(slot[:, 2 * u:2 * u + 2, w0:CH], ps[:, b:b + 2, w0:CH],
                                             ACT.Exp).then_inc(exp_done, 1)

            for c in range(NCH):
                with act.Fori(0, G) as g:
                    exps(c, g)

            def ln_act(l, n):
                act.wait_ge(ln_shift[l], n + 1)
                for j in range(TPC):
                    t = TPC * n + j
                    ins = nc.scalar.activation(xh[:, P * t:P * (t + 1)], x[:, t, :], ACT.Identity,
                                               bias=shift_by[:, n, j:j + 1], scale=rstd[:, n, j:j + 1])
                ins.then_inc(xh_ready[l], 1)

            def load_table(f):
                nc.scalar.activation(warm[:, 0:1], neghalf[:, 0:1], f)

            def relu(f, n):
                act.wait_ge(fk_psum, NCH * f + n + 1)
                nc.scalar.activation(relu_k[:, cols(n)], ps[:, high(n), :], ACT.Relu).then_inc(relu_ready, 1)

            def gate(f, n):
                act.wait_ge(fr_psum, NCH * f + n + 1)
                nc.scalar.activation(gate_r[:, cols(n)], ps[:, low(n), :], ACT.Sigmoid).then_inc(gate_ready, 1)

            def take_v(n):
                act.wait_ge(bv_psum, n + 1)
                nc.scalar.copy(vb[:, tiles(n), 0:D], ps[:, high(n), :].rearrange("p (t d) -> p t d", t=TPC)).then_inc(bv_ready, 1)

            def feature_parts(s, n):
                src, e, r = ((q_rot, q_exp, q_relu), (k_rot, k_exp, k_relu))[s]
                act.wait_ge(*((rot_ready, 2 * n + s + 1) if n < NCH - 1 else (rot_last, s + 1)))
                nc.scalar.activation(e[:, cols(n)], src[:, cols(n)], ACT.Exp).then_inc(feat_act, 1)
                nc.scalar.activation(r[:, cols(n)], src[:, cols(n)], ACT.Relu).then_inc(feat_act, 1)

            def turned_f(f, n):
                l = (LN2, LN4)[f]
                turned(xt_psum[l], xt_ready[l], n, low(n), xt_f[:, 1 + CH * n:1 + CH * (n + 1)])

            def last_gate(n):
                gate(0, n)
                if n == NCH - 1:
                    load_table(ACT.Exp)

            def turned_att(n):
                turned(att_psum, att_ready, n, low(n), att_t[:, cols(n)])

            load_table(ACT.Sigmoid)
            for n in range(NCH - 1):
                turned_att(n)
            ln_act(LN2, 0)
            turned_att(NCH - 1)
            turned_f(0, 0)
            in_turn(but_first(lambda n: ln_act(LN2, n)), but_first(lambda n: turned_f(0, n)), lambda n: relu(0, n), last_gate, None,
                    lambda n: ln_act(LN3, n),
                    lambda n: turned(xt_psum[LN3], xt_ready[LN3], n, low(n), xt_b[:, cols(n)]))
            trail(lambda n: [feature_parts(s, n) for s in range(2)], take_v)
            each(lambda n: turned(qft_psum, qft_ready, n, low(n), qft[:, cols(n)]),
                 lambda n: turned(nt_psum, nt_ready, n, low(n), att_t[:, cols(n)]))
            load_table(ACT.Sigmoid)
            in_turn(lambda n: ln_act(LN4, n), lambda n: turned_f(1, n), lambda n: relu(1, n), lambda n: gate(1, n))

        @block.vector
        def _(dve):
            steps = [0]

            def then(ins):
                steps[0] += 1
                ins.then_inc(dve_step, 1)
                dve.wait_ge(dve_step, steps[0])

            def ln_stats(l, n):
                for j in range(TPC):
                    steps[0] += 1
                    nc.vector.bn_stats(stats[:, n, j, :], x[:, TPC * n + j, :]).then_inc(dve_step, 1)
                for j in range(TPC):
                    dve.wait_ge(dve_step, steps[0] - TPC + 1 + j)
                    ins = nc.vector.bn_aggr(mv[:, n, j, :], stats[:, n, j, :])
                then(ins)
                nc.vector.tensor_scalar(negmean[:, n], mv[:, n, :, 0], -1.0, None, ALU.mult)
                nc.vector.tensor_scalar(veps[:, n], mv[:, n, :, 1], EPS, None, ALU.add).then_inc(ln_var[l], 1)

            def ln1_stats(n):
                dve.wait_ge(x_loaded[n], 16)
                ln_stats(LN1, n)

            def ln1_apply(n):
                if n % 2 == 0:
                    ln_apply(nc.vector, dve, LN1, n, xh_a[:, cols(n)])

            def split(n):
                for s, (pt, scale) in enumerate(((qparts, float(HD) ** -0.5), (kparts, 1.0))):
                    dve.wait_ge(hi_ready, 2 * n + s + 1)
                    if n >= 2:
                        dve.wait_ge(parts_ready, 2 * (n - 2) + s + 1)
                        dve.wait_ge(mid_ready, 2 * (n - 2) + s + 1)
                    nc.vector.scalar_tensor_tensor(res[:, n % 2, s], ps[:, 4 + 2 * s + n % 2, :], scale, pt[:, n, 0],
                                                   ALU.mult, ALU.subtract).then_inc(res_ready, 1)

            def low_parts(n):
                for s, pt in enumerate((qparts, kparts)):
                    dve.wait_ge(mid_ready, 2 * n + s + 1)
                    nc.vector.tensor_tensor(pt[:, n, 2], res[:, n % 2, s], pt[:, n, 1], ALU.subtract).then_inc(parts_ready, 1)

            trail(ln1_stats, ln1_apply)
            for n in range(NCH - 1):
                split(n)
                low_parts(n)
            split(NCH - 1)

            def stage_values(c, g, part):
                for a, b in runs(c, part):
                    ins = nc.vector.tensor_copy(vgrp[:, a:b, :], vaug[:, a:b, bass.ds(g * (4 * V1), 4 * V1)])
                ins.then_inc(v_staged, 1)

            dve.wait_ge(norm_psum, NCH)
            nc.vector.tensor_reduce(norms[:, :], ps[:, 2:4, :], AX.X, ALU.max).then_inc(bound_ready, 1)
            dve.wait_ge(all_max, 1)
            nc.vector.tensor_scalar(flag[0:1, 0:1], norms_all[0:1, 0:1], norms_all[0:1, 1:2], BOUND ** 2,
                                    ALU.mult, ALU.is_le).then_inc(flag_ready, 1)
            low_parts(NCH - 1)
            dve.wait_ge(w_loaded, 16)
            nc.vector.tensor_scalar(omu[:, :], w[:, MU_R:MU_K + 1], -1.0, 1.0, ALU.mult, ALU.add)
            nc.vector.memset(ot[:], 1.0).then_inc(ot_ready, 1)
            nc.vector.memset(o_inv[:], 1.0).then_inc(o_norm, 1)
            dve.wait_ge(ot_ready, 1)
            dve.wait_ge(o_norm, 1)
            dve.wait_ge(v_ready, NCH)
            stage_values(0, 0, 0)
            stage_values(0, 0, 1)

            dve.wait_ge(flag_ready, 1)
            small = dve.value_load(flag[0:1, 0:1], min_val=0, max_val=1)
            with dve.If(small == 0):
                nc.vector.memset(warm[:, 1:2], 0.0).then_inc(g_max, 2)
                for qb in range(TILES):
                    with dve.Fori(0, H // 2) as hp:
                        for i in range(2):
                            dve.wait_ge(g_scores, hp * 2 + (H * qb + i + 1))
                            row = qb // TPC * (H * TPC) + i * TPC + qb % TPC
                            nc.vector.tensor_reduce(negmax[:, bass.ds(hp * (2 * TPC) + row, 1)],
                                                    ps[:, 4 * i:4 * i + 4, :].rearrange("p b n -> p (b n)")[:, 0:(qb + 1) * P],
                                                    AX.X, ALU.max, negate=True).then_inc(g_max, 1)
                for a in range(2):
                    dve.wait_ge(g_turned, a + 1)
                    n1, n2, n3 = (nmp[:, a, j, :] for j in range(PARTS))
                    full, rest = nmt[:, a, 0, :], nmt[:, a, 1, :]
                    nc.vector.tensor_copy(full, ps[:, a, 0:P]).then_inc(g_step, 1)
                    dve.wait_ge(g_step, 4 * a + 1)
                    nc.vector.tensor_copy(n1, full).then_inc(g_step, 1)
                    dve.wait_ge(g_step, 4 * a + 2)
                    nc.vector.tensor_tensor(rest, full, n1, ALU.subtract).then_inc(g_step, 1)
                    dve.wait_ge(g_step, 4 * a + 3)
                    nc.vector.tensor_copy(n2, rest).then_inc(g_step, 1)
                    dve.wait_ge(g_step, 4 * a + 4)
                    nc.vector.tensor_tensor(n3, rest, n2, ALU.subtract).then_inc(g_parts, 1)

            def normalize(c, g):
                dve.wait_ge(o_turned, g + (G * c + 1))
                sums = ps[:, 7, :].rearrange("p (a r) -> p a r", r=32)
                nc.vector.reciprocal(o_inv[:], sums[:, :, HD]).then_inc(o_recip, 1)
                dve.wait_ge(o_recip, g + (G * c + 1))
                nc.vector.tensor_tensor(att[:, bass.ds(g * P + G * c * P, P)].rearrange("p (a v) -> p a v", v=HD), sums[:, :, 0:HD],
                                        o_inv[:].unsqueeze(2).broadcast_to([P, 4 * TPC, HD]), ALU.mult).then_inc(o_norm, 1)

            def group(c, g, nxt):
                k0 = g * kbs(c) + kbs_before(c)
                for i, (kb, w0) in enumerate(key_blocks(c)):
                    if kb < TPC * c:
                        continue
                    slot = probs_slot(i)[:, :, w0:w0 + P]
                    dve.wait_ge(exp_done, k0 * 2 + (3 + 2 * (i + 1)))
                    nc.vector.tensor_tensor(slot, slot, cs[:, C_TRI:C_TRI + P].unsqueeze(1).broadcast_to([P, 4, P]),
                                            ALU.min).then_inc(mask_done, 1)
                    if masked(c, i) == 3:
                        normalize(c, g)
                if nxt is not None and nxt[0] == c:
                    dve.wait_ge(pv_done, k0 + (4 + first_part(c)))
                    stage_values(*nxt, 0)
                dve.wait_ge(pv_done, k0 + (4 + kbs(c)))
                nc.vector.tensor_copy(ot[:], ps[:, 6, :]).then_inc(ot_ready, 1)
                if nxt is not None:
                    if nxt[0] != c:
                        stage_values(*nxt, 0)
                    stage_values(*nxt, 1)

            for c in range(NCH):
                with dve.Fori(0, G - 1) as g:
                    group(c, g, (c, g + 1))
                group(c, G - 1, (c + 1, 0) if c + 1 < NCH else None)

            nc.vector.memset(vb[:, :, D:D + 1], 1.0)
            nc.vector.memset(xt_f[:, 0:1], 0.0)
            nc.vector.tensor_scalar(w_mu[:, 0], w[:, W_KK:W_KK + D], w[:, MU_K:MU_K + 1], None, ALU.mult)
            nc.vector.tensor_scalar(w_mu[:, 1], w[:, W_KK:W_KK + D], omu[:, 1:2], None, ALU.mult).then_inc(mu_ready, 1)
            normalize(NCH, 0)

            def add_y(n):
                dve.wait_ge(x_again[n], 16)
                dve.wait_ge(y_psum, n + 1)
                nc.vector.tensor_tensor(x[:, tiles(n), :], ps[:, high(n), :].rearrange("p (t d) -> p t d", t=TPC), x[:, tiles(n), :],
                                        ALU.add).then_inc(y_added, 1)
                dve.wait_ge(y_added, n + 1)
                ln_stats(LN2, n)

            def mix_r(f, n):
                dve.wait_ge(shifted, NCH * f + n + 1)
                nc.vector.scalar_tensor_tensor(mix_rt[:, cols(n)], xt_f[:, 1 + CH * n:1 + CH * (n + 1)], w[:, MU_R:MU_R + 1],
                                               prev_r[:, cols(n)], ALU.mult, ALU.add).then_inc(mixed, 1)

            def k_squared(f, n):
                dve.wait_ge(relu_ready, NCH * f + n + 1)
                nc.vector.scalar_tensor_tensor(kact[:, cols(n)], ps[:, high(n), :], 0.0, relu_k[:, cols(n)],
                                               ALU.max, ALU.mult).then_inc(kact_ready, 1)

            def add_mix(f, n, l):
                dve.wait_ge(gate_ready, NCH * f + n + 1)
                dve.wait_ge(fv_psum, NCH * f + n + 1)
                then(nc.vector.tensor_tensor(gate_r[:, cols(n)], ps[:, high(n), :], gate_r[:, cols(n)], ALU.mult))
                nc.vector.tensor_tensor(x[:, tiles(n), :], x[:, tiles(n), :], gate_r[:, cols(n)].rearrange("p (t d) -> p t d", t=TPC),
                                        ALU.add).then_inc(f_added, 1)
                if l is not None:
                    dve.wait_ge(f_added, NCH * f + n + 1)
                    ln_stats(l, n)

            def rope(s, n):
                rot, tmp_all, bank, c_cos, c_sin = ((q_rot, q_tmp, high(n), C_CQ, C_SQ), (k_rot, k_tmp, low(n), C_CK, C_SK))[s]
                dve.wait_ge((bq_psum, bk_psum)[s], n + 1)
                a = ps[:, bank, :].rearrange("p (t h e) -> p t h e", t=TPC, h=H)
                cos, sin = (cs[:, c0 + HD * TPC * n:c0 + HD * TPC * (n + 1)].rearrange("p (t e) -> p t e", t=TPC).unsqueeze(2)
                            for c0 in (c_cos, c_sin))
                r, tmp = (z[:, cols(n)].rearrange("p (t h e) -> p t h e", t=TPC, h=H) for z in (rot, tmp_all))
                e = HD // 2
                nc.vector.tensor_tensor(r, a, cos.broadcast_to([P, TPC, H, HD]), ALU.mult)
                nc.vector.tensor_tensor(tmp[:, :, :, 0:e], a[:, :, :, e:], sin[:, :, :, 0:e].broadcast_to([P, TPC, H, e]), ALU.mult)
                nc.vector.tensor_tensor(tmp[:, :, :, e:], a[:, :, :, 0:e], sin[:, :, :, e:].broadcast_to([P, TPC, H, e]),
                                        ALU.mult).then_inc((rot_parts_q, rot_parts_k)[s], 1)
                if n == NCH - 1:
                    dve.wait_ge((rot_parts_q, rot_parts_k)[s], NCH)
                    nc.vector.tensor_tensor(rot[:, cols(n)], rot[:, cols(n)], tmp_all[:, cols(n)], ALU.add).then_inc(rot_last, 1)

            def features(n):
                for s, (e, r, feat) in enumerate(((q_exp, q_relu, q_feat), (k_exp, k_relu, k_feat))):
                    dve.wait_ge(feat_act, 4 * n + 2 * s + 2)
                    nc.vector.scalar_tensor_tensor(feat[:, cols(n)], e[:, cols(n)], 1.0, r[:, cols(n)],
                                                   ALU.min, ALU.add).then_inc(feat_ready, 1)

            each(add_y)
            trail(lambda n: (mix_r(0, n), k_squared(0, n)), lambda n: add_mix(0, n, LN3))
            for n in range(NCH + 2):
                if n < NCH:
                    rope(0, n)
                    rope(1, n)
                if n >= 2:
                    features(n - 2)

            dve.wait_ge(kv_psum, 1)
            nc.vector.tensor_tensor(kvb[:, 0:D], ps[:, high(0), 0:D], cs[:, C_BLK:C_BLK + D], ALU.mult)
            nc.vector.tensor_scalar(kvb[:, D:D + H], cs[:, C_HM:C_HM + H], ps[:, high(0), D:D + 1], None, ALU.mult).then_inc(kv_ready, 1)

            def divide(n):
                dve.wait_ge(n_psum, n + 1)
                sums = ps[:, 2 * n:2 * n + 2, :].rearrange("p b (u m) -> p (b u) m", u=2)
                inv = rden[:, TPC * H * n:TPC * H * (n + 1)].rearrange("p (t h) -> p t h", h=H)
                then(nc.vector.tensor_scalar(inv, sums[:, :, D:D + H], 1e-6, None, ALU.max))
                then(nc.vector.reciprocal(inv, inv))
                nc.vector.tensor_tensor(heads_out[:, cols(n)].rearrange("p (t h v) -> p t h v", t=TPC, v=HD),
                                        sums[:, :, 0:D].rearrange("p t (h v) -> p t h v", v=HD),
                                        inv.unsqueeze(3).broadcast_to([P, TPC, H, HD]), ALU.mult).then_inc(n_ready, 1)

            def add_y2(n):
                dve.wait_ge(y2_psum, n + 1)
                nc.vector.tensor_tensor(x[:, tiles(n), :], ps[:, high(n), :].rearrange("p (t d) -> p t d", t=TPC), x[:, tiles(n), :],
                                        ALU.add).then_inc(y2_added, 1)
                dve.wait_ge(y2_added, n + 1)
                ln_stats(LN4, n)

            each(divide,
                 add_y2)
            trail(lambda n: (mix_r(1, n), k_squared(1, n)), lambda n: add_mix(1, n, None))

        @block.tensor
        def _(pe):
            def turn(src, bank, done):
                for j in range(TPC):
                    ins = nc.tensor.transpose(ps[:, bank, P * j:P * (j + 1)], src[:, P * j:P * (j + 1)], ident)
                ins.then_inc(done, 1)

            def natural(bank, src, c0):
                for j in range(TPC):
                    ins = nc.tensor.matmul(ps[:, bank, P * j:P * (j + 1)], src[:, P * j:P * (j + 1)], w[:, c0:c0 + D],
                                           start=True, stop=True)
                return ins

            def turn_ln1(n):
                pe.wait_ge(ln1_ready[n], 1)
                at_least(pe, xt_ready[LN1], n)
                turn(xh_a[:, cols(n)], 0, xt_psum[LN1])

            def query_or_key(n, s):
                pe.wait_ge(xt_ready[LN1], n + 1)
                if n >= 2:
                    pe.wait_ge(res_ready, 2 * (n - 2) + s + 1)
                nc.tensor.matmul(ps[:, 4 + 2 * s + n % 2, :], w[:, (W_Q, W_K)[s]:(W_Q, W_K)[s] + D], xt_a[:, cols(n)],
                                 start=True, stop=True).then_inc(qk_psum, 1)

            def values(n):
                at_least(pe, v_ready, n - 1)
                natural(n % 2, xt_a[:, cols(n)], W_V).then_inc(v_psum, 1)

            pe.wait_ge(c_loaded, 16)
            nc.tensor.transpose(ps[:, 7, 0:P], ident, ident).then_inc(pv_done, 4)
            for _ in range(WARM_UP):
                nc.tensor.matmul(ps[:, 7, :], ident, cs[:, 0:CH], start=True, stop=True)
            pe.wait_ge(w_loaded, 16)

            def wait_rows(n):
                pe.wait_ge(const_loaded[n], CONST_LOADS)
                pe.wait_ge(qk_loaded[n], QK_LOADS)

            def square_norms(n):
                pe.wait_ge(hi_ready, 2 * n + 2)
                for s in range(2):
                    ins = nc.tensor.matmul(ps[32 * n:32 * (n + 1), 2 + s, :], cb[:, B_HN:B_HN + 32], sq[:, n % 2, s],
                                           start=True, stop=True)
                ins.then_inc(norm_psum, 1)

            turn_ln1(0)
            for n in range(NCH):
                query_or_key(n, 0)
                if n + 1 < NCH:
                    turn_ln1(n + 1)
                query_or_key(n, 1)
                if n == 0:
                    pe.wait_ge(cb_loaded, 16)
                else:
                    square_norms(n - 1)
            values(0)
            values(1)
            square_norms(NCH - 1)
            values(2)
            values(3)

            pe.wait_ge(flag_ready, 1)
            small = pe.value_load(flag[0:1, 0:1], min_val=0, max_val=1)
            with pe.If(small == 0):
                pe.wait_ge(v_ready, NCH)
                pe.wait_ge(first_loaded, QK_LOADS)
                for n in range(NCH):
                    wait_rows(n)
                for qb in range(TILES):
                    with pe.Fori(0, H // 2) as hp:
                        for i in range(2):
                            head = hp * (2 * CH) + i * CH
                            pe.wait_ge(g_max, hp * 2 + (H * qb + i + 1))
                            for k0 in range(0, (qb + 1) * P, CH):
                                k1 = min(k0 + CH, (qb + 1) * P)
                                bank = 4 * i + k0 // CH
                                ins = nc.tensor.matmul(ps[:, bank, 0:k1 - k0],
                                                       qq[0:SHIFT_ROW, bass.ds(head + (H * CH * (qb // TPC) + P * (qb % TPC)), P)],
                                                       kk[0:SHIFT_ROW, bass.ds(head + H * k0, k1 - k0)],
                                                       start=True, stop=True)
                            ins = nc.tensor.matmul(ps[:, bank, k1 - k0 - P:k1 - k0], cb[:, B_ID:B_ID + P], cb[:, B_TRI:B_TRI + P],
                                                   start=False, stop=True, skip_group_check=True)
                            ins.then_inc(g_scores, 1)
                pe.wait_ge(g_max, H * TILES + 2)
                for a in range(2):
                    nc.tensor.transpose(ps[:, a, 0:P], negmax[:, P * a:P * (a + 1)], ident).then_inc(g_turned, 1)
                pe.wait_ge(g_parts, 2)
                pe.wait_ge(g_rows, 16)

            def score(c, g, i, u):
                kb, w0 = key_blocks(c)[i]
                k0 = g * kbs(c) + kbs_before(c)
                n = 2 * i + u
                pe.wait_ge(exp_done, k0 * 2 + (n - back(c, n) + 4))
                for v in range(2):
                    head = g * (4 * CH) + (2 * u + v) * CH
                    ins = nc.tensor.matmul(ps[:, 2 * score_buffer(c, n) + v, w0:CH],
                                           kk[0:ROWS, bass.ds(head + (H * CH * (kb // TPC) + P * (kb % TPC)), P)],
                                           qq[0:ROWS, bass.ds(head + (H * CH * c + w0), CH - w0)], start=True, stop=True)
                ins.then_inc(s_done, 1)

            def weigh(c, g, i):
                kb, w0 = key_blocks(c)[i]
                k0 = g * kbs(c) + kbs_before(c)
                if i == 0:
                    pe.wait_ge(v_staged, g * 2 + (2 * G * c + 1))
                    pe.wait_ge(ot_ready, g + (G * c + 1))
                if i == first_part(c):
                    pe.wait_ge(v_staged, g * 2 + (2 * G * c + 2))
                pe.wait_ge(exp_done, k0 * 2 + (3 + 2 * (i + 1)))
                if kb >= TPC * c:
                    pe.wait_ge(mask_done, g * TPC + (TPC * G * c + masked(c, i)))
                for v in range(4):
                    ins = nc.tensor.matmul(ps[32 * v:32 * v + V1, 6, w0:CH], vgrp[:, kb, V1 * v:V1 * (v + 1)], probs_slot(i)[:, v, w0:CH],
                                           start=(i == 0), stop=(c == 0 or i == kbs(c) - 1), skip_group_check=True)
                ins.then_inc(pv_done, 1)

            def turn_sums(c, g):
                pe.wait_ge(ot_ready, g + (G * c + 1))
                pe.wait_ge(o_norm, g + (G * c + 1))
                for j in range(TPC):
                    ins = nc.tensor.transpose(ps[:, 7, P * j:P * (j + 1)], ot[:, P * j:P * (j + 1)], ident)
                ins.then_inc(o_turned, 1)

            def group(c, g, nxt):
                for i in range(2, kbs(c)):
                    score(c, g, i, 0)
                    weigh(c, g, i - 2)
                    score(c, g, i, 1)
                    if i == 2:
                        turn_sums(c, g)
                if nxt is not None and (c == 0 or nxt[0] != c):
                    wait_rows(nxt[0])
                for j in range(2):
                    if nxt is not None:
                        score(*nxt, j, 0)
                    weigh(c, g, kbs(c) - 2 + j)
                    if nxt is not None:
                        score(*nxt, j, 1)

            pe.wait_ge(v_ready, NCH)
            pe.wait_ge(res_ready, 2 * NCH)
            pe.wait_ge(bound_ready, 1)
            pe.wait_ge(const_loaded[0], CONST_LOADS)
            pe.wait_ge(first_loaded, QK_LOADS)
            for i in range(2):
                for u in range(2):
                    score(0, 0, i, u)
            for c in range(NCH):
                with pe.Fori(0, G - 1) as g:
                    group(c, g, (c, g + 1))
                group(c, G - 1, (c + 1, 0) if c + 1 < NCH else None)

            def stage(ready, free):
                for s, count in (ready, free):
                    at_least(pe, s, count)

            def turn_att(n):
                stage((o_norm, G * (n + 1) + 2), (exp_done, 3 + 2 * kbs_before(NCH)))
                for j in range(TPC):
                    for g in range(G):
                        a = P * (1 + G * n + g) + 32 * j
                        ins = nc.tensor.matmul(ps[32 * g:32 * (g + 1), low(n), P * j:P * (j + 1)], att[:, a:a + 32], ident,
                                               start=True, stop=True)
                ins.then_inc(att_psum, 1)

            def project(n):
                stage((att_ready, n + 1), (o_norm, G * NCH + 2) if n == NCH - 1 else (ot_ready, G * NCH + 1))
                natural(high(n), att_t[:, cols(n)], W_O).then_inc(y_psum, 1)

            def turn_ln2(n):
                stage((xh_ready[LN2], n + 1), (att_ready, n + 1))
                turn(xh[:, cols(n)], low(n), xt_psum[LN2])

            def mix_k_in(f, n):
                stage((xt_ready[(LN2, LN4)[f]], n + 1), ((y_added, y2_added)[f], n + 1))
                pe.wait_ge(mu_ready, 1)
                for i in range(2):
                    ins = nc.tensor.matmul(ps[:, high(n), :], w_mu[:, i], xt_f[:, CH * n + 1 - i:CH * (n + 1) + 1 - i],
                                           start=(i == 0), stop=(i == 1))
                ins.then_inc(fk_psum, 1)

            def mix_r_in(f, n):
                stage((mixed, NCH * f + n + 1), (xt_ready[(LN2, LN4)[f]], n + 1))
                ins = natural(low(n), mix_rt[:, cols(n)], W_R)
                ins.then_inc(fr_psum, 1)

            def mix_out(f, n):
                stage((kact_ready, NCH * f + n + 1), (kact_ready, NCH * f + n + 1))
                natural(high(n), kact[:, cols(n)], W_VV).then_inc(fv_psum, 1)

            def turn_ln3(n):
                stage((xh_ready[LN3], n + 1), (gate_ready, n + 1))
                turn(xh[:, cols(n)], low(n), xt_psum[LN3])

            def q_b(n):
                stage((xt_ready[LN3], n + 1), (f_added, n + 1))
                natural(high(n), xt_b[:, cols(n)], W_QKV).then_inc(bq_psum, 1)

            def k_b(n):
                stage((xt_ready[LN3], n + 1), (xt_ready[LN3], n + 1))
                natural(low(n), xt_b[:, cols(n)], W_QKV + D).then_inc(bk_psum, 1)

            def v_b(n):
                stage((xt_ready[LN3], n + 1), (rot_parts_q, n + 1))
                natural(high(n), xt_b[:, cols(n)], W_QKV + 2 * D).then_inc(bv_psum, 1)

            def turn_q(n):
                stage((feat_ready, 2 * n + 1), (rot_parts_k, n + 1))
                turn(q_feat[:, cols(n)], low(n), qft_psum)

            def summarize(n):
                stage((feat_ready, 2 * n + 2), (bv_ready, n + 1))
                for j in range(TPC):
                    t = TPC * n + j
                    ins = nc.tensor.matmul(ps[:, high(0), 0:D + 1], k_feat[:, P * t:P * (t + 1)], vb[:, t, :],
                                           start=(t == 0), stop=(t == TILES - 1))
                if n == NCH - 1:
                    ins.then_inc(kv_psum, 1)

            def numerators(n):
                stage((kv_ready, 1), (qft_ready, NCH))
                for j in range(TPC):
                    t = TPC * n + j
                    ins = nc.tensor.matmul(ps[:, t // 2, t % 2 * (CH // 2):t % 2 * (CH // 2) + D + H], qft[:, P * t:P * (t + 1)],
                                           kvb[:, 0:D + H], start=True, stop=True)
                ins.then_inc(n_psum, 1)

            def turn_heads(n):
                stage((n_ready, n + 1), (n_ready, n // 2 + 1))
                turn(heads_out[:, cols(n)], low(n), nt_psum)

            def project_b(n):
                stage((nt_ready, n + 1), (n_ready, high(n) // 2 + 1))
                natural(high(n), att_t[:, cols(n)], W_OUT).then_inc(y2_psum, 1)

            def turn_ln4(n):
                stage((xh_ready[LN4], n + 1), (nt_ready, n + 1))
                turn(xh[:, cols(n)], low(n), xt_psum[LN4])

            turn_att(0)
            turn_sums(NCH, 0)
            project(0)
            turn_att(1)
            for n in range(2, NCH):
                turn_att(n)
                project(n - 1)
            turn_ln2(0)
            project(NCH - 1)
            mix_k_in(0, 0)

            def keep_clock(count, bank):
                for _ in range(count):
                    nc.tensor.matmul(ps[:, bank, 0:2 * P], cb[:, B_ID:B_ID + P], cb[:, 0:2 * P], start=True, stop=True)

            def mix_rv(f, n):
                mix_r_in(f, n)
                mix_out(f, n)

            in_turn(but_first(turn_ln2), but_first(lambda n: mix_k_in(0, n)), lambda n: mix_rv(0, n), None, None, turn_ln3, lambda n: (q_b(n), k_b(n)))
            each(v_b, lambda n: (turn_q(n), summarize(n)),
                 numerators)
            for n in range(NCH - 1):
                turn_heads(n)
            project_b(0)
            project_b(1)
            turn_heads(NCH - 1)
            project_b(2)
            project_b(3)
            keep_clock(8, low(NCH - 1))
            turn_ln4(0)
            keep_clock(4, low(NCH - 1))
            in_turn(but_first(turn_ln4), lambda n: mix_k_in(1, n), lambda n: mix_rv(1, n))


def constants():
    f = np.float32

    def high(a):
        return (np.ascontiguousarray(a, f).view(np.uint32) & np.uint32(0xFFFF0000)).view(f)

    def bits(a):
        return (np.ascontiguousarray(a, f).view(np.uint32) >> np.uint32(16)).astype(np.uint16)

    c = np.zeros((P, N_C), f)
    c[:, C_ID:C_ID + P] = np.eye(P)
    k, q = np.arange(P)[:, None], np.arange(P)[None, :]
    c[:, C_TRI:C_TRI + P] = np.where(k <= q, f(3e38), f(0))
    c[:, C_BLK:C_BLK + P] = k // HD == q // HD
    c[:, C_HM:C_HM + H] = k // HD == np.arange(H)[None, :]
    inv = (1.0 / f(10000.0) ** (np.arange(0, HD, 2, dtype=f) / f(HD))).astype(f)
    ang = np.arange(T, dtype=f)[:, None] * inv[None, :]
    cos, sin = np.cos(ang), np.sin(ang)
    cos, sin = np.concatenate([cos, cos], 1), np.concatenate([-sin, sin], 1)
    for base, tab, s in ((C_CQ, cos, HD ** -0.5), (C_SQ, sin, HD ** -0.5), (C_CK, cos, 1.0), (C_SK, sin, 1.0)):
        c[:, base:base + TILES * HD] = (tab * f(s)).reshape(TILES, P, HD).transpose(1, 0, 2).reshape(P, -1)
    cb = np.zeros((P, N_B), f)
    cb[:, B_ID:B_ID + P] = np.eye(P)
    cb[:, B_TRI:B_TRI + P] = np.where(q > k, -1e30, 0.0)
    cb[:, B_HN:B_HN + H] = k % H == np.arange(H)[None, :]
    slopes = (f(1.0) / f(256.0) ** ((np.arange(H, dtype=f) + f(1)) / f(H))).astype(f)
    parts, rest = [], slopes
    for _ in range(PARTS):
        part = high(rest)
        parts.append(part)
        rest = rest - part
    pos = np.arange(T)
    hi, lo = pos // P * P, pos % P
    krows, qrows = np.zeros((CONST_ROWS, H, T), f), np.zeros((CONST_ROWS, H, T), f)
    for j, part in enumerate(parts):
        r = 4 * j
        krows[r], qrows[r] = hi[None, :], part[:, None]
        krows[r + 1], qrows[r + 1] = part[:, None], -hi[None, :]
        krows[r + 2], qrows[r + 2] = lo[None, :], part[:, None]
        krows[r + 3], qrows[r + 3] = part[:, None], -lo[None, :]
    krows[SHIFT_ROW - PAIR_ROWS:] = 1.0
    qrows[SHIFT_ROW - PAIR_ROWS] = -SHIFT
    krows, qrows = (r.reshape(CONST_ROWS, H, NCH, CH).transpose(0, 2, 1, 3).reshape(CONST_ROWS, H * T) for r in (krows, qrows))
    return c, bits(cb), bits(krows), bits(qrows)


def kernel(L0_attn_a_x, L0_attn_a_W_Q, L0_attn_a_W_K, L0_attn_a_W_V, L0_attn_a_W_O, L0_attn_b_w_qkv, L0_attn_b_w_out,
           L0_ffn_W_r, L0_ffn_W_k, L0_ffn_W_v, L0_ffn_mu_r, L0_ffn_mu_k):
    import concourse.bacc as bacc
    from concourse.bass_utils import run_bass_kernel_spmd

    nc = bacc.Bacc("TRN2", target_bir_lowering=False, num_devices=1)
    w_q, w_k = (np.asarray(m).reshape(H, HD, D).transpose(1, 0, 2).reshape(D, D) for m in (L0_attn_a_W_Q, L0_attn_a_W_K))
    weights = np.concatenate(
        [np.asarray(m).T for m in (w_q, w_k, L0_attn_a_W_V, L0_attn_a_W_O, L0_ffn_W_r, L0_ffn_W_k,
                                   L0_ffn_W_v, L0_attn_b_w_qkv, L0_attn_b_w_out)]
        + [np.asarray(L0_ffn_mu_r)[:, None], np.asarray(L0_ffn_mu_k)[:, None]], axis=1)
    consts, consts_b, krows, qrows = constants()
    arrays = {
        "in_x": np.ascontiguousarray(np.asarray(L0_attn_a_x).reshape(T, D)),
        "in_weights": np.ascontiguousarray(weights),
        "in_consts": consts, "in_consts_b": consts_b, "in_krows": krows, "in_qrows": qrows,
    }
    args = [nc.dram_tensor(name, a.shape, mybir.dt.from_np(a.dtype), kind="ExternalInput").ap() for name, a in arrays.items()]
    out = nc.dram_tensor("out_y", (T, D), F32, kind="ExternalOutput").ap()
    program(nc, *args, out)
    r = run_bass_kernel_spmd(nc, [arrays], core_ids=[0])
    return r.results[0]["out_y"].reshape(1, T, D)
```
